# Optimizing a Trainium2 kernel written in Bass

```python
import numpy as np
import jax
import jax.numpy as jnp

def _softmax(x, axis=-1):
    return jax.nn.softmax(x, axis=axis)

def _gelu(x):
    return jax.nn.gelu(x, approximate=True)

def _silu(x):
    return jax.nn.silu(x)

def _sigmoid(x):
    return jax.nn.sigmoid(x)

def _layernorm(x, axis=-1, eps=1e-05):
    m = jnp.mean(x, axis=axis, keepdims=True)
    v = jnp.var(x, axis=axis, keepdims=True)
    return (x - m) / jnp.sqrt(v + eps)

def _scatter_add(tgt, idx, src, axis=0):
    return tgt.at[idx].add(src)

def _segment_sum(src, seg, n):
    return jax.ops.segment_sum(src, seg, n)
kernel_name = 'mk_xattn_ffn_d1_seqx_r2_c2380f'

def setup_inputs(seed: int=0):
    np.random.seed(seed)
    _w = jnp.asarray

    def _rec_inputs():
        import jax
        import jax.numpy as jnp
        _rk = jax.random.key(seed)
        x = -0.0003929 + 0.9999 * jax.random.normal(jax.random.fold_in(_rk, 1), (8, 512, 2048), jnp.float32)
        _lenS = 512 - jax.random.randint(jax.random.fold_in(_rk, 7), (8,), 0, max(1, 512 // 4) + 1, jnp.int32)
        _lenS2 = 512 - jax.random.randint(jax.random.fold_in(_rk, 8), (8,), 0, max(1, 512 // 4) + 1, jnp.int32)
        _ctx_4096P = jax.random.normal(jax.random.fold_in(_rk, 11), (8, 16, 2048), jnp.float32)
        _ctx_4096c = jax.random.dirichlet(jax.random.fold_in(_rk, 511), 0.3 * jnp.ones((16,), jnp.float32), (8, 512))
        _ctx_4096t = jnp.einsum('bsk,bkd->bsd', _ctx_4096c, _ctx_4096P)
        _ctx_4096t = _ctx_4096t * jax.lax.rsqrt(jnp.mean(jnp.square(_ctx_4096t)) + 1e-12) * 0.953939
        ctx_4096 = 2.81802e-05 + 1.00001 * (_ctx_4096t + 0.3 * jax.random.normal(jax.random.fold_in(_rk, 611), (8, 512, 2048), jnp.float32))
        return (x, ctx_4096)
    x, ctx_4096 = _rec_inputs()

    def _L0_xattn_setup():
        import jax, jax.numpy as jnp
        import numpy as np
        EMB_DIM = 256
        HEADS = 8
        key = jax.random.key(seed)
        kq, kk, kv = jax.random.split(key, 3)
        B, C, N = (8, EMB_DIM, 2048)
        q = jax.random.normal(kq, (B, C, N), dtype=jnp.float32)
        k = jax.random.normal(kk, (B, C, N), dtype=jnp.float32)
        v = jax.random.normal(kv, (B, C, N), dtype=jnp.float32)
        return {'q': q, 'k': k, 'v': v}
    _L0_xattn_all = _L0_xattn_setup()
    _L0_xattn_in = {k: v for k, v in _L0_xattn_all.items() if k in ()}
    del _L0_xattn_all

    def _L0_ffn_setup():
        import jax, jax.numpy as jnp
        import numpy as np
        LORA_SCALE = 16.0 / jnp.sqrt(16.0)
        TOP_K = 2
        key = jax.random.key(seed)
        k1, k2, k3, k4 = jax.random.split(key, 4)
        B_, S, D, O, E, R = (4, 1024, 2048, 2048, 4, 16)
        x = jax.random.normal(k1, (B_, S, D), dtype=jnp.float32)
        router_w = jax.random.normal(k2, (E, D), dtype=jnp.float32) * 0.02
        A = jax.random.normal(k3, (E, R, D), dtype=jnp.float32) * 0.02
        B = jax.random.normal(k4, (O,), dtype=jnp.float32)
        B = jax.random.normal(k4, (E, O, R), dtype=jnp.float32) * 0.02
        return {'x': x, 'router_w': router_w, 'A': A, 'B': B}
    _L0_ffn_all = _L0_ffn_setup()
    _L0_ffn_in = {k: v for k, v in _L0_ffn_all.items() if k in ('router_w', 'A', 'B')}
    del _L0_ffn_all
    return {'x': x, 'ctx_4096': ctx_4096, 'L0_ffn_router_w': _L0_ffn_in['router_w'], 'L0_ffn_A': _L0_ffn_in['A'], 'L0_ffn_B': _L0_ffn_in['B']}

def reference(x, ctx_4096, L0_ffn_router_w, L0_ffn_A, L0_ffn_B):
    import jax
    import jax.numpy as jnp

    def _L0_xattn_ref(q, k, v):
        import jax, jax.numpy as jnp
        import numpy as np
        EMB_DIM = 256
        HEADS = 8
        B, C, N = q.shape
        H = HEADS
        dh = C // H
        qh = q.transpose(0, 2, 1).reshape(B, N, H, dh)
        kh = k.transpose(0, 2, 1).reshape(B, N, H, dh)
        vh = v.transpose(0, 2, 1).reshape(B, N, H, dh)
        qh = jax.nn.softmax(qh, axis=3)
        kh = jax.nn.softmax(kh, axis=1)
        kvs = jnp.einsum('bnhd,bnhe->bhde', kh, vh)
        out = jnp.einsum('bnhd,bhde->bnhe', qh, kvs)
        return out.transpose(0, 2, 3, 1).reshape(B, C, N)

    def _L0_ffn_ref(x, router_w, A, B):
        import jax, jax.numpy as jnp
        import numpy as np
        LORA_SCALE = 16.0 / jnp.sqrt(16.0)
        TOP_K = 2
        D = x.shape[-1]
        flat = x.reshape(-1, D)
        logits = flat @ router_w.T
        topk_vals, topk_idx = jax.lax.top_k(logits, TOP_K)
        sparse = jnp.full_like(logits, -jnp.inf)
        rows = jnp.arange(logits.shape[0])[:, None]
        sparse = sparse.at[rows, topk_idx].set(topk_vals)
        gates = jax.nn.softmax(sparse, axis=-1)
        mid = jnp.einsum('tf,erf->ter', flat, A)
        all_deltas = jnp.einsum('ter,eor->teo', mid, B) * LORA_SCALE
        delta = jnp.einsum('te,teo->to', gates, all_deltas)
        return delta.reshape(*x.shape[:-1], -1)
    x = x + _L0_xattn_ref(_layernorm(x, axis=-1), ctx_4096, ctx_4096)
    x = x + _L0_ffn_ref(_layernorm(x, axis=-1), L0_ffn_router_w, L0_ffn_A, L0_ffn_B)
    return x

_drawn_inputs = setup_inputs


def setup_inputs(seed=0):
    import zlib

    import numpy as np

    out = dict(_drawn_inputs(seed))
    spreads = {}
    factors = {}
    for name, (base, spread) in spreads.items():
        noise = np.random.default_rng([zlib.crc32(name.encode()), seed]).standard_normal(out[name].shape)
        drawn = base * np.exp(spread * noise) if base else spread * noise
        out[name] = jnp.asarray(drawn.astype(out[name].dtype))
    for name, factor in factors.items():
        out[name] = (out[name] * factor).astype(out[name].dtype)
    return out
```

```python
from contextlib import ExitStack

import concourse.bass as bass
from concourse import mybir

P = 128
ALU = mybir.AluOpType
ACT = mybir.ActivationFunctionType
AX = mybir.AxisListType
F32 = mybir.dt.float32
F32R = mybir.dt.float32r
BF16 = mybir.dt.bfloat16

EPS = 1e-5
LORA_SCALE = 4.0
RING = 4
G = 4
CH = 4
DH = 64


class Tile:

    def __init__(self, turn, c):
        self.turn, self.c = turn, c

    def __add__(self, n):
        return Tile(self.turn, self.c + n)

    def __sub__(self, n):
        return Tile(self.turn, self.c - n)

    def count(self, per_tile, more=0):
        return self.turn * (4 * per_tile) + (self.c * per_tile + more)

    def uses(self, by=1):
        return self.turn * by + (self.c // RING) * by

    @property
    def slot(self):
        return self.c % RING

    @property
    def par(self):
        return self.c % 2

    def live(self, tiles):
        return not isinstance(self.turn, int) or 0 <= 4 * self.turn + self.c < tiles


def after(eng, sem, value):
    if not isinstance(value, int) or value > 0:
        eng.wait_ge(sem, value)


def run_slots(nc, eng, first, last, loop_first, loop_last, body):
    turns = (loop_last - loop_first + 1) // 4
    for s in range(first, loop_first):
        body(Tile(0, s))
    with eng.Fori(0, turns) as turn:
        for j in range(4):
            body(Tile(turn, loop_first + j))
    for s in range(loop_first + 4 * turns, last + 1):
        body(Tile(0, s))


def xattn_lora_moe_kernel(nc, x, ctx_in, router_w, A, B, out):
    NB, C, N = x.shape
    E, R, _ = A.shape
    ER = E * R
    NT = NB * C // P
    NCH = N // P
    W = N // G
    NQ = 96
    assert NCH == G * CH and ER == 64 and ER + E <= NQ and W == 512 and P == 2 * DH

    x_rows = x.rearrange("b c n -> (b c) n")
    ctx_rows = ctx_in.rearrange("b c n -> (b c) n")
    out_rows = out.rearrange("b c n -> (b c) n")

    with ExitStack() as stack:
        def sb(name, shape, dt=F32):
            return stack.enter_context(nc.sbuf_tensor(name, shape, dt))

        def bank(name, shape=(P, 512)):
            return stack.enter_context(nc.psum_tensor(name, list(shape), F32))

        def sem(name):
            return stack.enter_context(nc.semaphore(name))

        ctx_sb = sb("ctx_sb", [P, RING, N])
        x_sb = sb("x_sb", [P, RING, N])
        x1_sb = sb("x1_sb", [P, RING, N])
        q_sb = sb("q_sb", [P, 2, N])
        vT = sb("vT", [P, 2, CH, P + 2])
        ekT = sb("ekT", [P, 2, CH, P])
        attnT = sb("attnT", [P, 2, CH, P])
        x1T = sb("x1T", [P, 2, CH, P])
        kv_bd = sb("kv_bd", [P, 2, 2 * (DH + 1)])
        rden = sb("rden", [P, 2, 2 * CH])
        junk = sb("junk", [P, 2, W], BF16)
        kmax_parts = sb("kmax_parts", [P, RING, G])
        kmax = sb("kmax", [P, RING])
        bn_parts = sb("bn_parts", [P, RING, G, 6])
        bn_out = sb("bn_out", [P, RING, 2])
        var1e = sb("var1e", [P, RING])
        rstd1 = sb("rstd1", [P, RING])
        nbias1 = sb("nbias1", [P, RING])
        rz = sb("rz", [P, RING])
        x1_sums = sb("x1_sums", [P, RING, G])
        x1_sum = sb("x1_sum", [P, RING])
        negmean2 = sb("negmean2", [P, RING])
        x1_sq = sb("x1_sq", [P, RING, G])
        var2 = sb("var2", [P, RING])
        var2e = sb("var2e", [P, RING])
        rstd2 = sb("rstd2", [P, RING])
        cen = sb("cen", [P, NQ])
        lmax = sb("lmax", [P, 1])
        lbias = sb("lbias", [P, 1])
        beats = sb("beats", [P, E, 2 * E])
        beats_m = sb("beats_m", [P, E, 2 * E])
        rank = sb("rank", [P, E])
        gexp = sb("gexp", [P, E])
        gsel = sb("gsel", [P, E])
        gsum = sb("gsum", [P, 1])
        grec = sb("grec", [P, 1])
        gscale = sb("gscale", [P, 1])
        mid = sb("mid", [P, ER])
        mid_hl = sb("mid_hl", [P, 2, ER], F32R)
        midT = sb("midT", [P, P], F32R)
        ident = sb("ident", [P, P])
        minus_half = sb("minus_half", [P, 1])
        ones = sb("ones", [P, P])
        order_mask = sb("order_mask", [P, E, 2 * E])
        w_rows = sb("w_rows", [NQ, N])
        wT = sb("wT", [P, NCH, NQ])
        w_sums = sb("w_sums", [P, NQ])
        b_rows = sb("b_rows", [P, E, NCH, R])
        b_twice = sb("b_twice", [P, NCH, 2, E, R])
        b_hi = sb("b_hi", [P, N], F32R)
        b_lo = sb("b_lo", [P, N], F32R)

        ctxT_ps = bank("ctxT_ps")
        attn_ps = bank("attn_ps")
        x1T_ps = bank("x1T_ps")
        delta_ps = bank("delta_ps")
        kv_ps = bank("kv_ps")
        raw_ps = bank("raw_ps")
        num_ps = bank("num_ps", (P, 2, 512))

        ctx_landed = [sem(f"ctx_landed{i}") for i in range(RING)]
        x_landed = [sem(f"x_landed{i}") for i in range(RING)]
        out_stored = [sem(f"out_stored{i}") for i in range(RING)]
        w_landed = sem("w_landed")
        r_landed = sem("r_landed")
        b_landed = [sem(f"b_landed{e}") for e in range(E)]
        ident_zeroed = sem("ident_zeroed")
        ident_made = sem("ident_made")
        pool_consts = sem("pool_consts")
        w_pad = sem("w_pad")
        wT_turned = sem("wT_turned")
        wT_copied = sem("wT_copied")
        w_summed = sem("w_summed")
        w_sums_copied = sem("w_sums_copied")
        b_twice_made = sem("b_twice_made")
        b_turned = sem("b_turned")
        b_hi_made = sem("b_hi_made")
        b_lo_made = sem("b_lo_made")
        ctxT_done = sem("ctxT_done")
        kv_done = sem("kv_done")
        num_done = sem("num_done")
        attn_done = sem("attn_done")
        x1T_done = sem("x1T_done")
        raw_done = sem("raw_done")
        midT_done = sem("midT_done")
        delta_done = sem("delta_done")
        kvT_made = sem("kvT_made")
        q_made = sem("q_made")
        x1T_copied = sem("x1T_copied")
        squares_made = sem("squares_made")
        gexp_made = sem("gexp_made")
        midT_copied = sem("midT_copied")
        kmax_parts_made = sem("kmax_parts_made")
        kmax_made = sem("kmax_made")
        bn_parts_made = sem("bn_parts_made")
        bn_made = sem("bn_made")
        var1e_made = sem("var1e_made")
        rstd1_made = sem("rstd1_made")
        nbias1_made = sem("nbias1_made")
        rz_made = sem("rz_made")
        kv_copied = sem("kv_copied")
        rden_made = sem("rden_made")
        attnT_made = sem("attnT_made")
        x1_made = sem("x1_made")
        x1_sum_made = sem("x1_sum_made")
        negmean2_made = sem("negmean2_made")
        var2_made = sem("var2_made")
        var2e_made = sem("var2e_made")
        rstd2_made = sem("rstd2_made")
        cen_made = sem("cen_made")
        lmax_made = sem("lmax_made")
        lbias_made = sem("lbias_made")
        beats_made = sem("beats_made")
        beats_masked = sem("beats_masked")
        rank_made = sem("rank_made")
        gsel_made = sem("gsel_made")
        grec_made = sem("grec_made")
        gscale_made = sem("gscale_made")
        mid_made = sem("mid_made")
        mid_hi_made = sem("mid_hi_made")
        mid_lo_made = sem("mid_lo_made")
        out_made = sem("out_made")
        ctx_shifted = sem("ctx_shifted")

        def cols(g):
            return slice(g * W, (g + 1) * W)

        POOL_CONSTS = 8 + 2 * (E - 1)

        block = stack.enter_context(nc.Block())

        @block.sync
        def _(sp):
            def load_ctx(t):
                sp.dma_start(ctx_sb[:, t.slot, :], ctx_rows[bass.ts(t.count(1), P), :]).then_inc(ctx_landed[t.slot], 16)

            def load_x(t):
                sp.dma_start(x_sb[:, t.slot, :], x_rows[bass.ts(t.count(1), P), :]).then_inc(x_landed[t.slot], 16)

            load_ctx(Tile(0, 0))
            load_x(Tile(0, 0))
            sp.dma_start(w_rows[0:ER, :], A.rearrange("e r n -> (e r) n")).then_inc(w_landed, 16)
            sp.wait_ge(w_pad, 1)
            sp.dma_start(w_rows[ER:ER + E, :], router_w).then_inc(r_landed, 16)
            load_ctx(Tile(0, 1))
            load_x(Tile(0, 1))
            for e in range(E):
                sp.dma_start(b_rows[:, e, :, :], B[e].rearrange("(p j) r -> p j r", j=NCH)).then_inc(b_landed[e], 16)
            for t in (2, 3):
                load_ctx(Tile(0, t))
                load_x(Tile(0, t))

            def slot(s):
                if (s + 4).live(NT):
                    if s.live(NT):
                        after(sp, ctxT_done, s.count(G, G))
                    load_ctx(s + 4)
                if (s + 3).live(NT) and (s - 1).live(NT):
                    after(sp, x1_made, (s - 1).count(G, G))
                    load_x(s + 3)
                if (s - 3).live(NT):
                    t = s - 3
                    after(sp, out_made, t.count(G, G))
                    sp.dma_start(out_rows[bass.ts(t.count(1), P), :], x1_sb[:, t.slot, :]).then_inc(out_stored[t.slot], 16)

            run_slots(nc, sp, 0, NT + 2, 4, NT - 5, slot)
            for i in range(RING):
                sp.wait_ge(out_stored[i], 16 * (NT // RING))

        @block.gpsimd
        def _(pool):
            pool.memset(ident[:], 0.0).then_inc(ident_zeroed, 1)
            pool.wait_ge(ident_zeroed, 1)
            pool.affine_select(out=ident[:], in_=ident[:], compare_op=ALU.not_equal, fill=1.0, base=0,
                               pattern=[[-1, P]], channel_multiplier=1).then_inc(ident_made, 1)
            pool.wait_ge(ident_made, 1)
            order = order_mask
            fills = [(ones[:], 1.0), (vT[:, 0, :, P:P + 2], 1.0), (vT[:, 1, :, P:P + 2], 1.0), (kv_bd[:], 0.0),
                     (minus_half[:], -0.5), (order[:], 0.0)]
            fills += [(kv_bd[h * DH:(h + 1) * DH, :, h * (DH + 1) + DH:h * (DH + 1) + DH + 1], 1.0) for h in range(2)]
            fills += [(order[:, e, e + 1:E], 1.0) for e in range(E - 1)]
            fills += [(order[:, e, E:E + e], 1.0) for e in range(1, E)]
            assert len(fills) == POOL_CONSTS
            for n, (what, value) in enumerate(fills):
                if n >= 1:
                    pool.wait_ge(pool_consts, n)
                pool.memset(what, value).then_inc(pool_consts, 1)

            def root(t, var, rstd, ready, made):
                if t.live(NT):
                    after(pool, ready, t.count(1, 1))
                    pool.tensor_tensor(rstd[:, t.slot:t.slot + 1], var[:, t.slot:t.slot + 1], minus_half[:],
                                       ALU.pow).then_inc(made, 1)

            def slot(s):
                root(s - 3, var2e, rstd2, var2e_made, rstd2_made)
                t = s + 1
                if t.live(NT):
                    after(pool, kmax_made, t.count(1, 1))
                    pool.tensor_tensor(ctx_sb[:, t.slot, :], ctx_sb[:, t.slot, :],
                                       kmax[:, t.slot:t.slot + 1].to_broadcast([P, N]),
                                       ALU.subtract).then_inc(ctx_shifted, 1)
                root(s + 1, var1e, rstd1, var1e_made, rstd1_made)

            run_slots(nc, pool, -1, NT + 2, 4, NT - 2, slot)

        @block.tensor
        def _(pe):
            pe.wait_ge(ident_made, 1)
            pe.wait_ge(w_landed, 16)
            pe.wait_ge(r_landed, 16)
            for g in range(G):
                if g >= 1:
                    pe.wait_ge(wT_copied, g)
                for j in range(CH):
                    c = g * CH + j
                    mm = pe.transpose(x1T_ps[:, j * NQ:(j + 1) * NQ], w_rows[:, c * P:(c + 1) * P], ident[0:NQ, 0:NQ])
                mm.then_inc(wT_turned, 1)
            pe.wait_ge(pool_consts, POOL_CONSTS)
            pe.wait_ge(wT_copied, G)
            for c in range(NCH):
                mm = pe.matmul(raw_ps[:, 0:NQ], ones[:], wT[:, c, :], start=(c == 0), stop=(c == NCH - 1))
            mm.then_inc(w_summed, 1)

            def turn_b():
                pe.wait_ge(b_twice_made, 2)
                for g in range(G):
                    if g >= 1:
                        pe.wait_ge(b_lo_made, g)
                    for j in range(CH):
                        mm = pe.transpose(delta_ps[:, j * P:(j + 1) * P],
                                          b_twice[:, g * CH + j, :, :, :].rearrange("p d e r -> p (d e r)"), ident[:])
                    mm.then_inc(b_turned, 1)

            def turn_ctx(t, g):
                if not t.live(NT):
                    return
                if g == 0:
                    after(pe, ctx_shifted, t.count(1, 1))
                after(pe, kvT_made, t.count(2 * G, 2 * g))
                for j in range(CH):
                    c = g * CH + j
                    mm = pe.transpose(ctxT_ps[:, j * P:(j + 1) * P], ctx_sb[:, t.slot, c * P:(c + 1) * P], ident[:])
                mm.then_inc(ctxT_done, 1)

            def kv(t, g):
                if not t.live(NT):
                    return
                if g == 0:
                    after(pe, kv_copied, t.count(2))
                after(pe, kvT_made, t.count(2 * G, 2 * g + 2))
                for j in range(CH):
                    mm = pe.matmul(kv_ps[:, 0:P + 2], ekT[:, g % 2, j, :], vT[:, g % 2, j, :],
                                   start=(g == 0 and j == 0), stop=(g == G - 1 and j == CH - 1))
                mm.then_inc(kv_done, 1)

            def numerator(t, g):
                if not t.live(NT):
                    return
                if g == 0:
                    after(pe, kv_copied, t.count(2, 2))
                after(pe, q_made, t.count(G, g + 1))
                after(pe, attnT_made, t.count(G, g))
                for j in range(CH):
                    c = g * CH + j
                    at = (j % 2) * 2 * (DH + 1)
                    mm = pe.matmul(num_ps[:, j // 2, at:at + 2 * (DH + 1)], q_sb[:, t.par, c * P:(c + 1) * P],
                                   kv_bd[:, t.par, :], start=True, stop=True)
                mm.then_inc(num_done, 1)

            def turn_attn(t, g):
                if not t.live(NT):
                    return
                after(pe, attnT_made, t.count(G, g + 1))
                after(pe, x1_made, t.count(G, g))
                for j in range(CH):
                    mm = pe.transpose(attn_ps[:, j * P:(j + 1) * P], attnT[:, g % 2, j, :], ident[:])
                mm.then_inc(attn_done, 1)

            def turn_x1(t, g):
                if not t.live(NT):
                    return
                after(pe, x1_made, t.count(G, g + 1))
                after(pe, x1T_copied, t.count(G, g))
                for j in range(CH):
                    c = g * CH + j
                    mm = pe.transpose(x1T_ps[:, j * P:(j + 1) * P], x1_sb[:, t.slot, c * P:(c + 1) * P], ident[:])
                mm.then_inc(x1T_done, 1)

            def project(t, g):
                if not t.live(NT):
                    return
                if g == 0:
                    after(pe, cen_made, t.count(1))
                after(pe, x1T_copied, t.count(G, g + 1))
                for j in range(CH):
                    mm = pe.matmul(raw_ps[:, 0:NQ], x1T[:, g % 2, j, :], wT[:, g * CH + j, :],
                                   start=(g == 0 and j == 0), stop=(g == G - 1 and j == CH - 1))
                mm.then_inc(raw_done, 1)

            def turn_mid(t):
                if not t.live(NT):
                    return
                after(pe, mid_lo_made, t.count(1, 1))
                after(pe, out_made, t.count(G))
                pe.transpose(delta_ps[:, 0:P], mid_hl[:].rearrange("p d m -> p (d m)").bitcast(F32),
                             ident[:]).then_inc(midT_done, 1)

            def delta(t, g):
                if not t.live(NT):
                    return
                after(pe, midT_copied, t.count(1, 1))
                after(pe, out_made, t.count(G, g))
                pe.matmul(delta_ps[:], midT[:], b_hi[:, cols(g)], start=True, stop=False)
                pe.matmul(delta_ps[:], midT[:], b_lo[:, cols(g)], start=False, stop=True).then_inc(delta_done, 1)

            def slot(s):
                if isinstance(s.turn, int) and s.c == 1:
                    turn_b()
                if isinstance(s.turn, int) and s.c == 3:
                    pe.wait_ge(b_lo_made, G)
                for g in range(G):
                    turn_ctx(s, g)
                    if g >= 1:
                        kv(s, g - 1)
                    turn_x1(s - 2, g)
                    if g >= 1:
                        project(s - 2, g - 1)
                        turn_attn(s - 1, g - 1)
                    if g == 1:
                        turn_mid(s - 3)
                    numerator(s - 1, g)
                    if g >= 1:
                        delta(s - 3, g - 1)
                kv(s, G - 1)
                project(s - 2, G - 1)
                turn_attn(s - 1, G - 1)
                delta(s - 3, G - 1)

            pe.wait_ge(w_sums_copied, 1)
            run_slots(nc, pe, 0, NT + 2, 4, NT - 1, slot)

        @block.scalar
        def _(act):
            for g in range(G):
                act.wait_ge(wT_turned, g + 1)
                act.activation(wT[:, g * CH:(g + 1) * CH, :],
                               x1T_ps[:, 0:CH * NQ].rearrange("p (j w) -> p j w", j=CH), ACT.Copy).then_inc(wT_copied, 1)
            act.wait_ge(w_summed, 1)
            act.activation(w_sums[:], raw_ps[:, 0:NQ], ACT.Copy).then_inc(w_sums_copied, 1)

            def b_parts():
                for g in range(G):
                    act.wait_ge(b_turned, g + 1)
                    act.activation(b_hi[:].rearrange("k (p j) -> k j p", j=NCH)[:, g * CH:(g + 1) * CH, :],
                                   delta_ps[:].rearrange("k (j p) -> k j p", j=CH), ACT.Copy).then_inc(b_hi_made, 1)

            def transposed_ctx(t, g):
                if not t.live(NT):
                    return
                after(act, ctxT_done, t.count(G, g + 1))
                after(act, kv_done, t.count(G, g - 1))
                act.activation(vT[:, g % 2, :, 0:P], ctxT_ps[:].rearrange("p (j c) -> p j c", j=CH),
                               ACT.Copy).then_inc(kvT_made, 1)
                act.activation(ekT[:, g % 2, :, :], ctxT_ps[:].rearrange("p (j c) -> p j c", j=CH),
                               ACT.Exp).then_inc(kvT_made, 1)

            def query(t, g):
                if not t.live(NT):
                    return
                if g == 0:
                    after(act, nbias1_made, t.count(1, 1))
                after(act, num_done, (t - 2).count(G, g + 1))
                act.activation(q_sb[:, t.par, cols(g)], x_sb[:, t.slot, cols(g)], ACT.Exp,
                               bias=nbias1[:, t.slot:t.slot + 1],
                               scale=rstd1[:, t.slot:t.slot + 1]).then_inc(q_made, 1)

            def copy_x1T(t, g):
                if not t.live(NT):
                    return
                after(act, x1T_done, t.count(G, g + 1))
                after(act, raw_done, t.count(G, g - 1))
                act.activation(x1T[:, g % 2, :, :], x1T_ps[:].rearrange("p (j c) -> p j c", j=CH),
                               ACT.Copy).then_inc(x1T_copied, 1)

            def square(t, g):
                if not t.live(NT):
                    return
                if g == 0:
                    after(act, negmean2_made, t.count(1, 1))
                after(act, squares_made, t.count(G, g - 1))
                act.activation(junk[:, g % 2, :], x1_sb[:, t.slot, cols(g)], ACT.Square,
                               bias=negmean2[:, t.slot:t.slot + 1],
                               accum_out=x1_sq[:, t.slot, g:g + 1]).then_inc(squares_made, 1)

            def gate_exp(t):
                if not t.live(NT):
                    return
                after(act, lbias_made, t.count(1, 1))
                act.activation(gexp[:], cen[:, ER:ER + E], ACT.Exp, bias=lbias[:, 0:1],
                               scale=rstd2[:, t.slot:t.slot + 1]).then_inc(gexp_made, 1)

            def copy_midT(t):
                if not t.live(NT):
                    return
                after(act, midT_done, t.count(1, 1))
                after(act, delta_done, t.count(G))
                act.activation(midT[:], delta_ps[:, 0:P], ACT.Copy).then_inc(midT_copied, 1)

            def slot(s):
                if isinstance(s.turn, int) and s.c == 1:
                    b_parts()
                for g in range(G):
                    transposed_ctx(s, g)
                    if g == 0:
                        gate_exp(s - 3)
                    copy_x1T(s - 2, g)
                    if g == 1:
                        copy_midT(s - 3)
                    query(s, g)
                    square(s - 2, g)

            act.wait_ge(pool_consts, POOL_CONSTS)
            run_slots(nc, act, 0, NT + 2, 4, NT - 1, slot)

        @block.vector
        def _(dve):
            def b_twice_parts():
                for e in range(E):
                    dve.wait_ge(b_landed[e], 16)
                for d in range(2):
                    dve.tensor_copy(b_twice[:, :, d, :, :], b_rows[:].rearrange("p e j r -> p j e r")).then_inc(b_twice_made, 1)

            def b_low():
                for g in range(G):
                    dve.wait_ge(b_hi_made, g + 1)
                    hi = b_hi[:].rearrange("k (p j) -> k j p", j=NCH)[:, g * CH:(g + 1) * CH, :]
                    lo = b_lo[:].rearrange("k (p j) -> k j p", j=NCH)[:, g * CH:(g + 1) * CH, :]
                    dve.tensor_tensor(lo, delta_ps[:].rearrange("k (j p) -> k j p", j=CH), hi,
                                      ALU.subtract).then_inc(b_lo_made, 1)

            def max_part(t, g):
                if not t.live(NT):
                    return
                if g == 0:
                    after(dve, ctx_landed[t.slot], t.uses(16) + 16)
                dve.tensor_reduce(kmax_parts[:, t.slot, g:g + 1], ctx_sb[:, t.slot, cols(g)], AX.X,
                                  ALU.max).then_inc(kmax_parts_made, 1)

            def max_whole(t):
                if not t.live(NT):
                    return
                after(dve, kmax_parts_made, t.count(G, G))
                dve.tensor_reduce(kmax[:, t.slot:t.slot + 1], kmax_parts[:, t.slot, :], AX.X,
                                  ALU.max).then_inc(kmax_made, 1)

            def bn_part(t, g):
                if not t.live(NT):
                    return
                if g == 0:
                    after(dve, x_landed[t.slot], t.uses(16) + 16)
                dve.bn_stats(bn_parts[:, t.slot, g, :], x_sb[:, t.slot, cols(g)]).then_inc(bn_parts_made, 1)

            def ln1(t, step):
                if not t.live(NT):
                    return
                i = t.slot
                if step == 0:
                    dve.bn_aggr(bn_out[:, i, :], bn_parts[:, i, :, :].rearrange("p g s -> p (g s)")).then_inc(bn_made, 1)
                if step == 1:
                    after(dve, bn_made, t.count(1, 1))
                    dve.tensor_scalar(var1e[:, i:i + 1], bn_out[:, i, 1:2], EPS, None, ALU.add).then_inc(var1e_made, 1)
                if step == 2:
                    after(dve, rstd1_made, t.count(1, 1))
                    dve.tensor_scalar(nbias1[:, i:i + 1], bn_out[:, i, 0:1], rstd1[:, i:i + 1], -1.0, ALU.mult,
                                      ALU.mult).then_inc(nbias1_made, 1)

            def kv_recip(t):
                if not t.live(NT):
                    return
                after(dve, kv_done, t.count(G, G))
                dve.reciprocal(rz[:, t.slot:t.slot + 1], kv_ps[:, P:P + 1]).then_inc(rz_made, 1)

            def copy_kv(t):
                if not t.live(NT):
                    return
                after(dve, rz_made, t.count(1, 1))
                after(dve, num_done, (t - 1).count(G))
                for h in range(2):
                    rows = slice(h * DH, (h + 1) * DH)
                    dve.tensor_scalar(kv_bd[rows, t.par, h * (DH + 1):h * (DH + 1) + DH], kv_ps[rows, h * DH:(h + 1) * DH],
                                      rz[rows, t.slot:t.slot + 1], None, ALU.mult).then_inc(kv_copied, 1)

            def normalise(t, g):
                if not t.live(NT):
                    return
                heads = num_ps[:, :, 0:4 * (DH + 1)].rearrange("p b (k w) -> p b k w", w=DH + 1)
                after(dve, num_done, t.count(G, g + 1))
                dve.reciprocal(rden[:, :, 0:CH], heads[:, :, :, DH]).then_inc(rden_made, 1)
                after(dve, rden_made, t.count(G, g + 1))
                after(dve, attn_done, t.count(G, g - 1))
                dve.tensor_tensor(attnT[:, g % 2, :, :].rearrange("p (b j) (h d) -> p b (j h) d", b=2, h=2),
                                  heads[:, :, :, 0:DH],
                                  rden[:, :, 0:CH].unsqueeze(3).to_broadcast([P, 2, CH, DH]),
                                  ALU.mult).then_inc(attnT_made, 1)

            def add_x(t, g):
                if not t.live(NT):
                    return
                if g == 0:
                    after(dve, out_stored[t.slot], t.uses(16))
                after(dve, attn_done, t.count(G, g + 1))
                dve.scalar_tensor_tensor(out=x1_sb[:, t.slot, cols(g)], in0=attn_ps[:], scalar=kmax[:, t.slot:t.slot + 1],
                                         in1=x_sb[:, t.slot, cols(g)], op0=ALU.add, op1=ALU.add,
                                         accum_out=x1_sums[:, t.slot, g:g + 1]).then_inc(x1_made, 1)

            def mean2(t, step):
                if not t.live(NT):
                    return
                i = t.slot
                if step == 0:
                    after(dve, x1_made, t.count(G, G))
                    dve.tensor_reduce(x1_sum[:, i:i + 1], x1_sums[:, i, :], AX.X, ALU.add).then_inc(x1_sum_made, 1)
                if step == 1:
                    after(dve, x1_sum_made, t.count(1, 1))
                    dve.tensor_scalar(negmean2[:, i:i + 1], x1_sum[:, i:i + 1], -1.0 / N, None,
                                      ALU.mult).then_inc(negmean2_made, 1)

            def gates_in(t):
                if not t.live(NT):
                    return
                i = t.slot
                lg = cen[:, ER:ER + E]
                after(dve, squares_made, t.count(G, G))
                dve.tensor_reduce(var2[:, i:i + 1], x1_sq[:, i, :], AX.X, ALU.add).then_inc(var2_made, 1)
                after(dve, raw_done, t.count(G, G))
                dve.scalar_tensor_tensor(out=cen[:], in0=w_sums[:], scalar=negmean2[:, i:i + 1], in1=raw_ps[:, 0:NQ],
                                         op0=ALU.mult, op1=ALU.add).then_inc(cen_made, 1)
                after(dve, var2_made, t.count(1, 1))
                dve.tensor_scalar(var2e[:, i:i + 1], var2[:, i:i + 1], 1.0 / N, EPS, ALU.mult,
                                  ALU.add).then_inc(var2e_made, 1)
                after(dve, cen_made, t.count(1, 1))
                dve.tensor_reduce(lmax[:], lg, AX.X, ALU.max).then_inc(lmax_made, 1)
                them = lg.unsqueeze(1).to_broadcast([P, E, E])
                it = lg.unsqueeze(2).to_broadcast([P, E, E])
                dve.tensor_tensor(beats[:, :, 0:E], them, it, ALU.is_gt).then_inc(beats_made, 1)
                after(dve, rstd2_made, t.count(1, 1))
                after(dve, lmax_made, t.count(1, 1))
                dve.tensor_scalar(lbias[:], lmax[:], rstd2[:, i:i + 1], -1.0, ALU.mult, ALU.mult).then_inc(lbias_made, 1)
                dve.tensor_tensor(beats[:, :, E:2 * E], them, it, ALU.is_ge).then_inc(beats_made, 1)
                after(dve, beats_made, t.count(2, 2))
                dve.tensor_tensor(beats_m[:], beats[:], order_mask[:], ALU.mult).then_inc(beats_masked, 1)
                after(dve, beats_masked, t.count(1, 1))
                dve.tensor_reduce(rank[:], beats_m[:], AX.X, ALU.add).then_inc(rank_made, 1)

            def gates_out(t):
                if not t.live(NT):
                    return
                i = t.slot
                after(dve, rank_made, t.count(1, 1))
                after(dve, gexp_made, t.count(1, 1))
                dve.scalar_tensor_tensor(out=gsel[:], in0=rank[:], scalar=2.0, in1=gexp[:], op0=ALU.is_lt,
                                         op1=ALU.mult, accum_out=gsum[:]).then_inc(gsel_made, 1)
                after(dve, gsel_made, t.count(1, 1))
                dve.reciprocal(grec[:], gsum[:]).then_inc(grec_made, 1)
                after(dve, grec_made, t.count(1, 1))
                dve.tensor_scalar(gscale[:], grec[:], rstd2[:, i:i + 1], LORA_SCALE, ALU.mult,
                                  ALU.mult).then_inc(gscale_made, 1)
                after(dve, gscale_made, t.count(1, 1))
                dve.scalar_tensor_tensor(out=mid[:].rearrange("p (e r) -> p e r", e=E),
                                         in0=cen[:, 0:ER].rearrange("p (e r) -> p e r", e=E), scalar=gscale[:, 0:1],
                                         in1=gsel[:].unsqueeze(2).to_broadcast([P, E, R]),
                                         op0=ALU.mult, op1=ALU.mult).then_inc(mid_made, 1)
                after(dve, mid_made, t.count(1, 1))
                after(dve, midT_done, t.count(1))
                dve.tensor_copy(mid_hl[:, 0, :], mid[:]).then_inc(mid_hi_made, 1)
                after(dve, mid_hi_made, t.count(1, 1))
                dve.tensor_tensor(mid_hl[:, 1, :], mid[:], mid_hl[:, 0, :], ALU.subtract).then_inc(mid_lo_made, 1)

            def add_delta(t, g):
                if not t.live(NT):
                    return
                after(dve, delta_done, t.count(G, g + 1))
                dve.tensor_tensor(x1_sb[:, t.slot, cols(g)], delta_ps[:], x1_sb[:, t.slot, cols(g)],
                                  ALU.add).then_inc(out_made, 1)

            def slot(s):
                early = isinstance(s.turn, int)
                if early and s.c == 1:
                    b_low()
                for g in range(G):
                    if g == 0:
                        gates_in(s - 3)
                    normalise(s - 1, g)
                    if g == 0:
                        gates_out(s - 3)
                    if g >= 1:
                        add_x(s - 1, g - 1)
                    max_part(s + 2, g)
                    bn_part(s + 1, g)
                    if g >= 1:
                        add_delta(s - 3, g - 1)
                kv_recip(s)
                if (s + 1).live(NT):
                    after(dve, bn_parts_made, (s + 1).count(G, G))
                max_whole(s + 2)
                ln1(s + 1, 0)
                copy_kv(s)
                ln1(s + 1, 1)
                add_x(s - 1, G - 1)
                mean2(s - 1, 0)
                add_delta(s - 3, G - 1)
                mean2(s - 1, 1)
                ln1(s + 1, 2)
                if early and s.c == -1:
                    b_twice_parts()
                    dve.wait_ge(pool_consts, POOL_CONSTS)
                    dve.wait_ge(w_sums_copied, 1)

            dve.memset(w_rows[ER:NQ, :], 0.0).then_inc(w_pad, 1)
            run_slots(nc, dve, -2, NT + 2, 5, NT - 3, slot)


_INS = ["x", "ctx_4096", "L0_ffn_router_w", "L0_ffn_A", "L0_ffn_B"]
_OUTS = [((8, 512, 2048), "float32")]


def kernel(**inputs):
    import numpy as _np
    import concourse.bacc as _bacc
    from concourse import mybir as _mybir
    from concourse.bass_utils import run_bass_kernel_spmd as _run

    nc = _bacc.Bacc("TRN2", target_bir_lowering=False, num_devices=1)
    arrays, args = {}, []
    for name in _INS:
        a = _np.ascontiguousarray(inputs[name])
        arrays[f"in_{name}_dram"] = a
        args.append(nc.dram_tensor(f"in_{name}_dram", a.shape, _mybir.dt.from_np(a.dtype), kind="ExternalInput").ap())
    for i, (shape, dtype) in enumerate(_OUTS):
        dt = _mybir.dt.from_np(_np.dtype(dtype))
        args.append(nc.dram_tensor(f"out_{i}_dram", shape, dt, kind="ExternalOutput").ap())
    xattn_lora_moe_kernel(nc, *args)
    r = _run(nc, [arrays], core_ids=[0])
    return r.results[0]["out_0_dram"]
```

```python
from contextlib import ExitStack

import concourse.bass as bass
from concourse import mybir

P = 128
ALU = mybir.AluOpType
ACT = mybir.ActivationFunctionType
AX = mybir.AxisListType
F32 = mybir.dt.float32
F32R = mybir.dt.float32r
BF16 = mybir.dt.bfloat16

EPS = 1e-5
LORA_SCALE = 4.0
RING = 4
G = 4
CH = 4
DH = 64


class Tile:

    def __init__(self, turn, c):
        self.turn, self.c = turn, c

    def __add__(self, n):
        return Tile(self.turn, self.c + n)

    def __sub__(self, n):
        return Tile(self.turn, self.c - n)

    def count(self, per_tile, more=0):
        return self.turn * (4 * per_tile) + (self.c * per_tile + more)

    def uses(self, by=1):
        return self.turn * by + (self.c // RING) * by

    @property
    def slot(self):
        return self.c % RING

    @property
    def par(self):
        return self.c % 2

    def live(self, tiles):
        return not isinstance(self.turn, int) or 0 <= 4 * self.turn + self.c < tiles


def after(eng, sem, value):
    if not isinstance(value, int) or value > 0:
        eng.wait_ge(sem, value)


def run_slots(nc, eng, first, last, loop_first, loop_last, body):
    turns = (loop_last - loop_first + 1) // 4
    for s in range(first, loop_first):
        body(Tile(0, s))
    with eng.Fori(0, turns) as turn:
        for j in range(4):
            body(Tile(turn, loop_first + j))
    for s in range(loop_first + 4 * turns, last + 1):
        body(Tile(0, s))


def xattn_lora_moe_kernel(nc, x, ctx_in, router_w, A, B, out):
    NB, C, N = x.shape
    E, R, _ = A.shape
    ER = E * R
    NT = NB * C // P
    NCH = N // P
    W = N // G
    NQ = 96
    assert NCH == G * CH and ER == 64 and ER + E <= NQ and W == 512 and P == 2 * DH

    x_rows = x.rearrange("b c n -> (b c) n")
    ctx_rows = ctx_in.rearrange("b c n -> (b c) n")
    out_rows = out.rearrange("b c n -> (b c) n")

    with ExitStack() as stack:
        def sb(name, shape, dt=F32):
            return stack.enter_context(nc.sbuf_tensor(name, shape, dt))

        def bank(name, shape=(P, 512)):
            return stack.enter_context(nc.psum_tensor(name, list(shape), F32))

        def sem(name):
            return stack.enter_context(nc.semaphore(name))

        ctx_sb = sb("ctx_sb", [P, RING, N])
        x_sb = sb("x_sb", [P, RING, N])
        x1_sb = sb("x1_sb", [P, RING, N])
        q_sb = sb("q_sb", [P, 2, N])
        vT = sb("vT", [P, 2, CH, P + 2])
        ekT = sb("ekT", [P, 2, CH, P])
        attnT = sb("attnT", [P, 2, CH, P])
        x1T = sb("x1T", [P, 2, CH, P])
        kv_bd = sb("kv_bd", [P, 2, 2 * (DH + 1)])
        rden = sb("rden", [P, 2, CH])
        junk = sb("junk", [P, 2, W], BF16)
        kmax_parts = sb("kmax_parts", [P, RING, G])
        kmax = sb("kmax", [P, RING])
        bn_parts = sb("bn_parts", [P, RING, G, 6])
        bn_out = sb("bn_out", [P, RING, 2])
        var1e = sb("var1e", [P, RING])
        rstd1 = sb("rstd1", [P, RING])
        nbias1 = sb("nbias1", [P, RING])
        rz = sb("rz", [P, RING])
        x1_sums = sb("x1_sums", [P, RING, G])
        x1_sum = sb("x1_sum", [P, RING])
        negmean2 = sb("negmean2", [P, RING])
        x1_sq = sb("x1_sq", [P, RING, G])
        var2 = sb("var2", [P, RING])
        var2e = sb("var2e", [P, RING])
        rstd2 = sb("rstd2", [P, RING])
        cen = sb("cen", [P, NQ])
        lmax = sb("lmax", [P, 1])
        lbias = sb("lbias", [P, 1])
        beats = sb("beats", [P, E, 2 * E])
        beats_m = sb("beats_m", [P, E, 2 * E])
        rank = sb("rank", [P, E])
        gexp = sb("gexp", [P, E])
        gsel = sb("gsel", [P, E])
        gsum = sb("gsum", [P, 1])
        grec = sb("grec", [P, 1])
        cen_scaled = sb("cen_scaled", [P, ER])
        mid = sb("mid", [P, ER])
        mid_hl = sb("mid_hl", [P, 2, ER], F32R)
        midT = sb("midT", [P, P], F32R)
        ident = sb("ident", [P, P])
        minus_half = sb("minus_half", [P, 1])
        ones = sb("ones", [P, P])
        order_mask = sb("order_mask", [P, E, 2 * E])
        w_rows = sb("w_rows", [NQ, N])
        wT = sb("wT", [P, NCH, NQ])
        w_sums = sb("w_sums", [P, NQ])
        b_rows = sb("b_rows", [P, E, NCH, R])
        b_twice = sb("b_twice", [P, NCH, 2, E, R])
        b_hi = sb("b_hi", [P, N], F32R)
        b_lo = sb("b_lo", [P, N], F32R)

        ctxT_ps = bank("ctxT_ps")
        attn_ps = bank("attn_ps")
        x1T_ps = bank("x1T_ps")
        delta_ps = bank("delta_ps")
        kv_ps = bank("kv_ps")
        raw_ps = bank("raw_ps")
        num_ps = bank("num_ps", (P, 2, 512))
        spare = [x1T_ps, delta_ps, raw_ps]

        ctx_landed = [sem(f"ctx_landed{i}") for i in range(RING)]
        x_landed = [sem(f"x_landed{i}") for i in range(RING)]
        out_stored = [sem(f"out_stored{i}") for i in range(RING)]
        w_landed = sem("w_landed")
        r_landed = sem("r_landed")
        b_landed = [sem(f"b_landed{e}") for e in range(E)]
        ident_zeroed = sem("ident_zeroed")
        ident_made = sem("ident_made")
        pool_consts = sem("pool_consts")
        w_pad = sem("w_pad")
        wT_turned = sem("wT_turned")
        wT_copied = sem("wT_copied")
        w_summed = sem("w_summed")
        w_sums_copied = sem("w_sums_copied")
        b_twice_made = sem("b_twice_made")
        b_turned = sem("b_turned")
        b_hi_made = sem("b_hi_made")
        b_lo_made = sem("b_lo_made")
        ctxT_done = sem("ctxT_done")
        kv_done = sem("kv_done")
        num_done = sem("num_done")
        attn_done = sem("attn_done")
        x1T_done = sem("x1T_done")
        raw_done = sem("raw_done")
        midT_done = sem("midT_done")
        delta_done = sem("delta_done")
        kvT_made = sem("kvT_made")
        q_made = sem("q_made")
        x1T_copied = sem("x1T_copied")
        squares_made = sem("squares_made")
        gexp_made = sem("gexp_made")
        midT_copied = sem("midT_copied")
        kmax_parts_made = sem("kmax_parts_made")
        kmax_made = sem("kmax_made")
        bn_parts_made = sem("bn_parts_made")
        bn_made = sem("bn_made")
        var1e_made = sem("var1e_made")
        rstd1_made = sem("rstd1_made")
        nbias1_made = sem("nbias1_made")
        rz_made = sem("rz_made")
        kv_copied = sem("kv_copied")
        rden_made = sem("rden_made")
        attnT_made = sem("attnT_made")
        x1_made = sem("x1_made")
        x1_sum_made = sem("x1_sum_made")
        negmean2_made = sem("negmean2_made")
        var2_made = sem("var2_made")
        var2e_made = sem("var2e_made")
        rstd2_made = sem("rstd2_made")
        cen_made = sem("cen_made")
        lmax_made = sem("lmax_made")
        lbias_made = sem("lbias_made")
        beats_made = sem("beats_made")
        beats_masked = sem("beats_masked")
        rank_made = sem("rank_made")
        gsel_made = sem("gsel_made")
        grec_made = sem("grec_made")
        cen_scaled_made = sem("cen_scaled_made")
        mid_made = sem("mid_made")
        mid_hi_made = sem("mid_hi_made")
        mid_lo_made = sem("mid_lo_made")
        out_made = sem("out_made")
        ctx_shifted = sem("ctx_shifted")

        def cols(g):
            return slice(g * W, (g + 1) * W)

        POOL_CONSTS = 8 + 2 * (E - 1)

        block = stack.enter_context(nc.Block())

        @block.sync
        def _(sp):
            def load_ctx(t):
                sp.dma_start(ctx_sb[:, t.slot, :], ctx_rows[bass.ts(t.count(1), P), :]).then_inc(ctx_landed[t.slot], 16)

            def load_x(t):
                sp.dma_start(x_sb[:, t.slot, :], x_rows[bass.ts(t.count(1), P), :]).then_inc(x_landed[t.slot], 16)

            load_ctx(Tile(0, 0))
            load_ctx(Tile(0, 1))
            load_x(Tile(0, 0))
            sp.dma_start(w_rows[0:ER, :], A.rearrange("e r n -> (e r) n")).then_inc(w_landed, 16)
            sp.wait_ge(w_pad, 1)
            sp.dma_start(w_rows[ER:ER + E, :], router_w).then_inc(r_landed, 16)
            load_ctx(Tile(0, 2))
            load_x(Tile(0, 1))
            for e in range(E):
                sp.dma_start(b_rows[:, e, :, :], B[e].rearrange("(p j) r -> p j r", j=NCH)).then_inc(b_landed[e], 16)
            load_ctx(Tile(0, 3))
            load_x(Tile(0, 2))
            load_x(Tile(0, 3))

            def slot(s):
                if (s - 4).live(NT):
                    t = s - 4
                    after(sp, out_made, t.count(G, G))
                    sp.dma_start(out_rows[bass.ts(t.count(1), P), :], x1_sb[:, t.slot, :]).then_inc(out_stored[t.slot], 16)
                if (s + 4).live(NT):
                    if s.live(NT):
                        after(sp, ctxT_done, s.count(G, G))
                    load_ctx(s + 4)
                if (s + 3).live(NT) and (s - 1).live(NT):
                    after(sp, x1_made, (s - 1).count(G, G))
                    load_x(s + 3)

            run_slots(nc, sp, 0, NT + 3, 4, NT - 5, slot)
            for i in range(RING):
                sp.wait_ge(out_stored[i], 16 * (NT // RING))

        @block.gpsimd
        def _(pool):
            pool.memset(ident[:], 0.0).then_inc(ident_zeroed, 1)
            pool.wait_ge(ident_zeroed, 1)
            pool.affine_select(out=ident[:], in_=ident[:], compare_op=ALU.not_equal, fill=1.0, base=0,
                               pattern=[[-1, P]], channel_multiplier=1).then_inc(ident_made, 1)
            pool.wait_ge(ident_made, 1)
            order = order_mask
            fills = [(ones[:], 1.0), (vT[:, 0, :, P:P + 2], 1.0), (vT[:, 1, :, P:P + 2], 1.0), (kv_bd[:], 0.0),
                     (minus_half[:], -0.5), (order[:], 0.0)]
            fills += [(kv_bd[h * DH:(h + 1) * DH, :, h * (DH + 1) + DH:h * (DH + 1) + DH + 1], 1.0) for h in range(2)]
            fills += [(order[:, e, e + 1:E], 1.0) for e in range(E - 1)]
            fills += [(order[:, e, E:E + e], 1.0) for e in range(1, E)]
            assert len(fills) == POOL_CONSTS
            for n, (what, value) in enumerate(fills):
                if n >= 1:
                    pool.wait_ge(pool_consts, n)
                pool.memset(what, value).then_inc(pool_consts, 1)

            def root(t, var, rstd, ready, made):
                if t.live(NT):
                    after(pool, ready, t.count(1, 1))
                    pool.tensor_tensor(rstd[:, t.slot:t.slot + 1], var[:, t.slot:t.slot + 1], minus_half[:],
                                       ALU.pow).then_inc(made, 1)

            def slot(s):
                root(s - 3, var2e, rstd2, var2e_made, rstd2_made)
                t = s + 1
                if t.live(NT) and not (isinstance(t.turn, int) and t.c == 0):
                    after(pool, kmax_made, t.count(1, 1))
                    pool.tensor_tensor(ctx_sb[:, t.slot, :], ctx_sb[:, t.slot, :],
                                       kmax[:, t.slot:t.slot + 1].to_broadcast([P, N]),
                                       ALU.subtract).then_inc(ctx_shifted, 1)
                root(s + 1, var1e, rstd1, var1e_made, rstd1_made)

            run_slots(nc, pool, -1, NT + 2, 4, NT - 2, slot)

        @block.tensor
        def _(pe):
            pe.wait_ge(ident_made, 1)
            def turn_w():
                pe.wait_ge(w_landed, 16)
                pe.wait_ge(r_landed, 16)
                for g in range(G):
                    if g >= 3:
                        pe.wait_ge(wT_copied, g - 2)
                    for j in range(CH):
                        c = g * CH + j
                        mm = pe.transpose(spare[g % 3][:, j * NQ:(j + 1) * NQ], w_rows[:, c * P:(c + 1) * P],
                                          ident[0:NQ, 0:NQ])
                    mm.then_inc(wT_turned, 1)

            def sum_w():
                pe.wait_ge(pool_consts, POOL_CONSTS)
                pe.wait_ge(wT_copied, G)
                for c in range(NCH):
                    mm = pe.matmul(raw_ps[:, 0:NQ], ones[:], wT[:, c, :], start=(c == 0), stop=(c == NCH - 1))
                mm.then_inc(w_summed, 1)

            def turn_b(g):
                if g == 0:
                    pe.wait_ge(b_twice_made, 2)
                    pe.wait_ge(wT_copied, G)
                if g >= 2:
                    pe.wait_ge(b_lo_made, g - 1)
                for j in range(CH):
                    mm = pe.transpose(spare[g % 2][:, j * P:(j + 1) * P],
                                      b_twice[:, g * CH + j, :, :, :].rearrange("p d e r -> p (d e r)"), ident[:])
                mm.then_inc(b_turned, 1)

            def turn_ctx(t, g):
                if not t.live(NT):
                    return
                if g == 0:
                    after(pe, ctx_shifted, t.count(1, 1))
                after(pe, kvT_made, t.count(2 * G, 2 * g))
                for j in range(CH):
                    c = g * CH + j
                    mm = pe.transpose(ctxT_ps[:, j * P:(j + 1) * P], ctx_sb[:, t.slot, c * P:(c + 1) * P], ident[:])
                mm.then_inc(ctxT_done, 1)

            def kv(t, g):
                if not t.live(NT):
                    return
                if g == 0:
                    after(pe, kv_copied, t.count(2))
                after(pe, kvT_made, t.count(2 * G, 2 * g + 2))
                for j in range(CH):
                    mm = pe.matmul(kv_ps[:, 0:P + 2], ekT[:, g % 2, j, :], vT[:, g % 2, j, :],
                                   start=(g == 0 and j == 0), stop=(g == G - 1 and j == CH - 1))
                mm.then_inc(kv_done, 1)

            def numerator(t, g):
                if not t.live(NT):
                    return
                if g == 0:
                    after(pe, kv_copied, t.count(2, 2))
                after(pe, q_made, t.count(G, g + 1))
                after(pe, attnT_made, t.count(G, g))
                for j in range(CH):
                    c = g * CH + j
                    at = (j % 2) * 2 * (DH + 1)
                    mm = pe.matmul(num_ps[:, j // 2, at:at + 2 * (DH + 1)], q_sb[:, t.par, c * P:(c + 1) * P],
                                   kv_bd[:, t.par, :], start=True, stop=True)
                mm.then_inc(num_done, 1)

            def turn_attn(t, g):
                if not t.live(NT):
                    return
                after(pe, attnT_made, t.count(G, g + 1))
                after(pe, x1_made, t.count(G, g))
                for j in range(CH):
                    mm = pe.transpose(attn_ps[:, j * P:(j + 1) * P], attnT[:, g % 2, j, :], ident[:])
                mm.then_inc(attn_done, 1)

            def turn_x1(t, g):
                if not t.live(NT):
                    return
                after(pe, x1_made, t.count(G, g + 1))
                after(pe, x1T_copied, t.count(G, g))
                for j in range(CH):
                    c = g * CH + j
                    mm = pe.transpose(x1T_ps[:, j * P:(j + 1) * P], x1_sb[:, t.slot, c * P:(c + 1) * P], ident[:])
                mm.then_inc(x1T_done, 1)

            def project(t, g):
                if not t.live(NT):
                    return
                if g == 0:
                    after(pe, cen_made, t.count(1))
                after(pe, x1T_copied, t.count(G, g + 1))
                for j in range(CH):
                    mm = pe.matmul(raw_ps[:, 0:NQ], x1T[:, g % 2, j, :], wT[:, g * CH + j, :],
                                   start=(g == 0 and j == 0), stop=(g == G - 1 and j == CH - 1))
                mm.then_inc(raw_done, 1)

            def turn_mid(t):
                if not t.live(NT):
                    return
                after(pe, mid_lo_made, t.count(1, 1))
                after(pe, out_made, t.count(G))
                pe.transpose(delta_ps[:, 0:P], mid_hl[:].rearrange("p d m -> p (d m)").bitcast(F32),
                             ident[:]).then_inc(midT_done, 1)

            def delta(t, g):
                if not t.live(NT):
                    return
                after(pe, midT_copied, t.count(1, 1))
                after(pe, out_made, t.count(G, g))
                pe.matmul(delta_ps[:], midT[:], b_hi[:, cols(g)], start=True, stop=False)
                pe.matmul(delta_ps[:], midT[:], b_lo[:, cols(g)], start=False, stop=True).then_inc(delta_done, 1)

            def slot(s):
                early = isinstance(s.turn, int)
                if early and s.c == 1:
                    turn_w()
                    turn_b(0)
                    turn_b(1)
                if early and s.c == 2:
                    pe.wait_ge(w_sums_copied, 1)
                    pe.wait_ge(b_lo_made, G)
                for g in range(G):
                    turn_ctx(s, g)
                    if g >= 1:
                        kv(s, g - 1)
                    turn_x1(s - 2, g)
                    if g >= 1:
                        project(s - 2, g - 1)
                        turn_attn(s - 1, g - 1)
                    if g == 2:
                        turn_mid(s - 3)
                    numerator(s - 1, g)
                    if g == 0:
                        delta(s - 4, G - 1)
                    if g >= 2:
                        delta(s - 3, g - 2)
                kv(s, G - 1)
                project(s - 2, G - 1)
                turn_attn(s - 1, G - 1)
                delta(s - 3, G - 2)
                if early and s.c == 1:
                    turn_b(2)
                    turn_b(3)
                    sum_w()

            run_slots(nc, pe, 0, NT + 3, 4, NT - 1, slot)

        @block.scalar
        def _(act):
            def copy_wT():
                for g in range(G):
                    act.wait_ge(wT_turned, g + 1)
                    act.activation(wT[:, g * CH:(g + 1) * CH, :],
                                   spare[g % 3][:, 0:CH * NQ].rearrange("p (j w) -> p j w", j=CH),
                                   ACT.Copy).then_inc(wT_copied, 1)

            def copy_w_sums():
                act.wait_ge(w_summed, 1)
                act.activation(w_sums[:], raw_ps[:, 0:NQ], ACT.Copy).then_inc(w_sums_copied, 1)

            def b_high(g):
                act.wait_ge(b_turned, g + 1)
                act.activation(b_hi[:].rearrange("k (p j) -> k j p", j=NCH)[:, g * CH:(g + 1) * CH, :],
                               spare[g % 2][:].rearrange("k (j p) -> k j p", j=CH), ACT.Copy).then_inc(b_hi_made, 1)

            def transposed_ctx(t, g):
                if not t.live(NT):
                    return
                after(act, ctxT_done, t.count(G, g + 1))
                after(act, kv_done, t.count(G, g - 1))
                act.activation(vT[:, g % 2, :, 0:P], ctxT_ps[:].rearrange("p (j c) -> p j c", j=CH),
                               ACT.Copy).then_inc(kvT_made, 1)
                act.activation(ekT[:, g % 2, :, :], ctxT_ps[:].rearrange("p (j c) -> p j c", j=CH),
                               ACT.Exp).then_inc(kvT_made, 1)

            def query(t, g):
                if not t.live(NT):
                    return
                if g == 0:
                    after(act, nbias1_made, t.count(1, 1))
                after(act, num_done, (t - 2).count(G, g + 1))
                act.activation(q_sb[:, t.par, cols(g)], x_sb[:, t.slot, cols(g)], ACT.Exp,
                               bias=nbias1[:, t.slot:t.slot + 1],
                               scale=rstd1[:, t.slot:t.slot + 1]).then_inc(q_made, 1)

            def copy_x1T(t, g):
                if not t.live(NT):
                    return
                after(act, x1T_done, t.count(G, g + 1))
                after(act, raw_done, t.count(G, g - 1))
                act.activation(x1T[:, g % 2, :, :], x1T_ps[:].rearrange("p (j c) -> p j c", j=CH),
                               ACT.Copy).then_inc(x1T_copied, 1)

            def square(t, g):
                if not t.live(NT):
                    return
                if g == 0:
                    after(act, negmean2_made, t.count(1, 1))
                after(act, squares_made, t.count(G, g - 1))
                act.activation(junk[:, g % 2, :], x1_sb[:, t.slot, cols(g)], ACT.Square,
                               bias=negmean2[:, t.slot:t.slot + 1],
                               accum_out=x1_sq[:, t.slot, g:g + 1]).then_inc(squares_made, 1)

            def copy_kv(t):
                if not t.live(NT):
                    return
                after(act, rz_made, t.count(1, 1))
                after(act, num_done, (t - 1).count(G))
                for h in range(2):
                    rows = slice(h * DH, (h + 1) * DH)
                    act.activation(kv_bd[rows, t.par, h * (DH + 1):h * (DH + 1) + DH], kv_ps[rows, h * DH:(h + 1) * DH],
                                   ACT.Copy, scale=rz[rows, t.slot:t.slot + 1]).then_inc(kv_copied, 1)

            def gate_exp(t):
                if not t.live(NT):
                    return
                after(act, lbias_made, t.count(1, 1))
                act.activation(gexp[:], cen[:, ER:ER + E], ACT.Exp, bias=lbias[:, 0:1],
                               scale=rstd2[:, t.slot:t.slot + 1]).then_inc(gexp_made, 1)

            def copy_midT(t):
                if not t.live(NT):
                    return
                after(act, midT_done, t.count(1, 1))
                after(act, delta_done, t.count(G))
                act.activation(midT[:], delta_ps[:, 0:P], ACT.Copy).then_inc(midT_copied, 1)

            def slot(s):
                early = isinstance(s.turn, int)
                if early and s.c == 1:
                    copy_wT()
                    b_high(0)
                    b_high(1)
                for g in range(G):
                    transposed_ctx(s, g)
                    copy_x1T(s - 2, g)
                    if g == 2:
                        copy_midT(s - 3)
                    query(s, g)
                    if g == 0:
                        gate_exp(s - 3)
                    square(s - 2, g)
                copy_kv(s)
                if early and s.c == 1:
                    b_high(2)
                    b_high(3)
                    copy_w_sums()

            act.wait_ge(pool_consts, POOL_CONSTS)
            run_slots(nc, act, 0, NT + 2, 4, NT - 1, slot)

        @block.vector
        def _(dve):
            def b_twice_parts():
                for e in range(E):
                    dve.wait_ge(b_landed[e], 16)
                for d in range(2):
                    dve.tensor_copy(b_twice[:, :, d, :, :], b_rows[:].rearrange("p e j r -> p j e r")).then_inc(b_twice_made, 1)

            def b_low(groups):
                for g in groups:
                    dve.wait_ge(b_hi_made, g + 1)
                    both = spare[g % 2]
                    hi = b_hi[:].rearrange("k (p j) -> k j p", j=NCH)[:, g * CH:(g + 1) * CH, :]
                    lo = b_lo[:].rearrange("k (p j) -> k j p", j=NCH)[:, g * CH:(g + 1) * CH, :]
                    dve.tensor_tensor(lo, both[:].rearrange("k (j p) -> k j p", j=CH), hi,
                                      ALU.subtract).then_inc(b_lo_made, 1)

            def max_part(t, g):
                if not t.live(NT):
                    return
                if g == 0:
                    after(dve, ctx_landed[t.slot], t.uses(16) + 16)
                dve.tensor_reduce(kmax_parts[:, t.slot, g:g + 1], ctx_sb[:, t.slot, cols(g)], AX.X,
                                  ALU.max).then_inc(kmax_parts_made, 1)

            def max_whole(t):
                if not t.live(NT):
                    return
                after(dve, kmax_parts_made, t.count(G, G))
                dve.tensor_reduce(kmax[:, t.slot:t.slot + 1], kmax_parts[:, t.slot, :], AX.X,
                                  ALU.max).then_inc(kmax_made, 1)

            def bn_part(t, g):
                if not t.live(NT):
                    return
                if g == 0:
                    after(dve, x_landed[t.slot], t.uses(16) + 16)
                dve.bn_stats(bn_parts[:, t.slot, g, :], x_sb[:, t.slot, cols(g)]).then_inc(bn_parts_made, 1)

            def ln1(t, step):
                if not t.live(NT):
                    return
                i = t.slot
                if step == 0:
                    dve.bn_aggr(bn_out[:, i, :], bn_parts[:, i, :, :].rearrange("p g s -> p (g s)")).then_inc(bn_made, 1)
                if step == 1:
                    after(dve, bn_made, t.count(1, 1))
                    dve.tensor_scalar(var1e[:, i:i + 1], bn_out[:, i, 1:2], EPS, None, ALU.add).then_inc(var1e_made, 1)
                if step == 2:
                    after(dve, rstd1_made, t.count(1, 1))
                    dve.tensor_scalar(nbias1[:, i:i + 1], bn_out[:, i, 0:1], rstd1[:, i:i + 1], -1.0, ALU.mult,
                                      ALU.mult).then_inc(nbias1_made, 1)

            def kv_recip(t):
                if (t + 1).live(NT):
                    after(dve, bn_parts_made, (t + 1).count(G, G))
                if not t.live(NT):
                    return
                after(dve, kv_done, t.count(G, G))
                dve.reciprocal(rz[:, t.slot:t.slot + 1], kv_ps[:, P:P + 1]).then_inc(rz_made, 1)

            heads = num_ps[:, :, 0:4 * (DH + 1)].rearrange("p b (k w) -> p b k w", w=DH + 1)

            def den_recip(t, g):
                if not t.live(NT):
                    return
                after(dve, num_done, t.count(G, g + 1))
                dve.reciprocal(rden[:], heads[:, :, :, DH]).then_inc(rden_made, 1)

            def normalise(t, g):
                if not t.live(NT):
                    return
                after(dve, rden_made, t.count(G, g + 1))
                after(dve, attn_done, t.count(G, g - 1))
                dve.tensor_tensor(attnT[:, g % 2, :, :].rearrange("p (b j) (h d) -> p b (j h) d", b=2, h=2),
                                  heads[:, :, :, 0:DH], rden[:].unsqueeze(3).to_broadcast([P, 2, CH, DH]),
                                  ALU.mult).then_inc(attnT_made, 1)

            def add_x(t, g):
                if not t.live(NT):
                    return
                if g == 0:
                    after(dve, out_stored[t.slot], t.uses(16))
                after(dve, attn_done, t.count(G, g + 1))
                dve.scalar_tensor_tensor(out=x1_sb[:, t.slot, cols(g)], in0=attn_ps[:], scalar=kmax[:, t.slot:t.slot + 1],
                                         in1=x_sb[:, t.slot, cols(g)], op0=ALU.add, op1=ALU.add,
                                         accum_out=x1_sums[:, t.slot, g:g + 1]).then_inc(x1_made, 1)

            def mean2(t, step):
                if not t.live(NT):
                    return
                i = t.slot
                if step == 0:
                    after(dve, x1_made, t.count(G, G))
                    dve.tensor_reduce(x1_sum[:, i:i + 1], x1_sums[:, i, :], AX.X, ALU.add).then_inc(x1_sum_made, 1)
                if step == 1:
                    after(dve, x1_sum_made, t.count(1, 1))
                    dve.tensor_scalar(negmean2[:, i:i + 1], x1_sum[:, i:i + 1], -1.0 / N, None,
                                      ALU.mult).then_inc(negmean2_made, 1)

            def gate(t, step):
                if not t.live(NT):
                    return
                i = t.slot
                lg = cen[:, ER:ER + E]
                them = lg.unsqueeze(1).to_broadcast([P, E, E])
                it = lg.unsqueeze(2).to_broadcast([P, E, E])
                if step == "variance sum":
                    after(dve, squares_made, t.count(G, G))
                    dve.tensor_reduce(var2[:, i:i + 1], x1_sq[:, i, :], AX.X, ALU.add).then_inc(var2_made, 1)
                if step == "centre":
                    after(dve, raw_done, t.count(G, G))
                    dve.scalar_tensor_tensor(out=cen[:], in0=w_sums[:], scalar=negmean2[:, i:i + 1],
                                             in1=raw_ps[:, 0:NQ], op0=ALU.mult, op1=ALU.add).then_inc(cen_made, 1)
                if step == "variance":
                    after(dve, var2_made, t.count(1, 1))
                    dve.tensor_scalar(var2e[:, i:i + 1], var2[:, i:i + 1], 1.0 / N, EPS, ALU.mult,
                                      ALU.add).then_inc(var2e_made, 1)
                if step == "logit maximum":
                    after(dve, cen_made, t.count(1, 1))
                    dve.tensor_reduce(lmax[:], lg, AX.X, ALU.max).then_inc(lmax_made, 1)
                if step == "greater":
                    dve.tensor_tensor(beats[:, :, 0:E], them, it, ALU.is_gt).then_inc(beats_made, 1)
                if step == "logit bias":
                    after(dve, rstd2_made, t.count(1, 1))
                    after(dve, lmax_made, t.count(1, 1))
                    dve.tensor_scalar(lbias[:], lmax[:], rstd2[:, i:i + 1], -1.0, ALU.mult,
                                      ALU.mult).then_inc(lbias_made, 1)
                if step == "greater or equal":
                    dve.tensor_tensor(beats[:, :, E:2 * E], them, it, ALU.is_ge).then_inc(beats_made, 1)
                if step == "mask":
                    after(dve, beats_made, t.count(2, 2))
                    dve.tensor_tensor(beats_m[:], beats[:], order_mask[:], ALU.mult).then_inc(beats_masked, 1)
                if step == "rank":
                    after(dve, beats_masked, t.count(1, 1))
                    dve.tensor_reduce(rank[:], beats_m[:], AX.X, ALU.add).then_inc(rank_made, 1)
                if step == "select":
                    after(dve, rank_made, t.count(1, 1))
                    after(dve, gexp_made, t.count(1, 1))
                    dve.scalar_tensor_tensor(out=gsel[:], in0=rank[:], scalar=2.0, in1=gexp[:], op0=ALU.is_lt,
                                             op1=ALU.mult, accum_out=gsum[:]).then_inc(gsel_made, 1)
                if step == "over sum":
                    after(dve, gsel_made, t.count(1, 1))
                    dve.reciprocal(grec[:], gsum[:]).then_inc(grec_made, 1)
                if step == "scaled middle":
                    dve.tensor_scalar(cen_scaled[:], cen[:, 0:ER], rstd2[:, i:i + 1], LORA_SCALE, ALU.mult,
                                      ALU.mult).then_inc(cen_scaled_made, 1)
                if step == "middle":
                    after(dve, cen_scaled_made, t.count(1, 1))
                    after(dve, grec_made, t.count(1, 1))
                    dve.scalar_tensor_tensor(out=mid[:].rearrange("p (e r) -> p e r", e=E),
                                             in0=cen_scaled[:].rearrange("p (e r) -> p e r", e=E),
                                             scalar=grec[:, 0:1], in1=gsel[:].unsqueeze(2).to_broadcast([P, E, R]),
                                             op0=ALU.mult, op1=ALU.mult).then_inc(mid_made, 1)
                if step == "high part":
                    after(dve, mid_made, t.count(1, 1))
                    after(dve, midT_done, t.count(1))
                    dve.tensor_copy(mid_hl[:, 0, :], mid[:]).then_inc(mid_hi_made, 1)
                if step == "low part":
                    after(dve, mid_hi_made, t.count(1, 1))
                    dve.tensor_tensor(mid_hl[:, 1, :], mid[:], mid_hl[:, 0, :], ALU.subtract).then_inc(mid_lo_made, 1)

            def add_delta(t, g):
                if not t.live(NT):
                    return
                after(dve, delta_done, t.count(G, g + 1))
                dve.tensor_tensor(x1_sb[:, t.slot, cols(g)], delta_ps[:], x1_sb[:, t.slot, cols(g)],
                                  ALU.add).then_inc(out_made, 1)

            def slot(s):
                early = isinstance(s.turn, int)
                if early and s.c == 1:
                    b_low((0, 1))
                gate(s - 3, "variance sum")
                gate(s - 3, "centre")
                ln1(s, 2)
                gate(s - 3, "variance")
                gate(s - 3, "logit maximum")
                gate(s - 3, "greater")
                den_recip(s - 1, 0)
                max_part(s + 2, 0)
                normalise(s - 1, 0)
                gate(s - 3, "logit bias")
                gate(s - 3, "greater or equal")
                gate(s - 3, "scaled middle")
                add_delta(s - 4, G - 1)
                gate(s - 3, "mask")
                bn_part(s + 1, 0)
                gate(s - 3, "rank")
                add_x(s - 1, 0)
                gate(s - 3, "select")
                den_recip(s - 1, 1)
                gate(s - 3, "over sum")
                normalise(s - 1, 1)
                gate(s - 3, "middle")
                gate(s - 3, "high part")
                max_part(s + 2, 1)
                gate(s - 3, "low part")
                add_x(s - 1, 1)
                bn_part(s + 1, 1)
                den_recip(s - 1, 2)
                max_part(s + 2, 2)
                normalise(s - 1, 2)
                add_delta(s - 3, 0)
                max_part(s + 2, 3)
                bn_part(s + 1, 2)
                add_x(s - 1, 2)
                den_recip(s - 1, 3)
                max_whole(s + 2)
                bn_part(s + 1, 3)
                normalise(s - 1, 3)
                add_delta(s - 3, 1)
                kv_recip(s)
                ln1(s + 1, 0)
                add_x(s - 1, 3)
                ln1(s + 1, 1)
                mean2(s - 1, 0)
                add_delta(s - 3, 2)
                mean2(s - 1, 1)
                if early and s.c == -2:
                    dve.wait_ge(kmax_made, 1)
                    dve.tensor_scalar(ctx_sb[:, 0, :], ctx_sb[:, 0, :], kmax[:, 0:1], None,
                                      ALU.subtract).then_inc(ctx_shifted, 1)
                if early and s.c == 0:
                    b_twice_parts()
                if early and s.c == 1:
                    b_low((2, 3))
                    dve.wait_ge(pool_consts, POOL_CONSTS)
                    dve.wait_ge(w_sums_copied, 1)

            dve.memset(w_rows[ER:NQ, :], 0.0).then_inc(w_pad, 1)
            run_slots(nc, dve, -2, NT + 3, 5, NT - 3, slot)


_INS = ["x", "ctx_4096", "L0_ffn_router_w", "L0_ffn_A", "L0_ffn_B"]
_OUTS = [((8, 512, 2048), "float32")]


def kernel(**inputs):
    import numpy as _np
    import concourse.bacc as _bacc
    from concourse import mybir as _mybir
    from concourse.bass_utils import run_bass_kernel_spmd as _run

    nc = _bacc.Bacc("TRN2", target_bir_lowering=False, num_devices=1)
    arrays, args = {}, []
    for name in _INS:
        a = _np.ascontiguousarray(inputs[name])
        arrays[f"in_{name}_dram"] = a
        args.append(nc.dram_tensor(f"in_{name}_dram", a.shape, _mybir.dt.from_np(a.dtype), kind="ExternalInput").ap())
    for i, (shape, dtype) in enumerate(_OUTS):
        dt = _mybir.dt.from_np(_np.dtype(dtype))
        args.append(nc.dram_tensor(f"out_{i}_dram", shape, dt, kind="ExternalOutput").ap())
    xattn_lora_moe_kernel(nc, *args)
    r = _run(nc, [arrays], core_ids=[0])
    return r.results[0]["out_0_dram"]
```

```python
from contextlib import ExitStack

import concourse.bass as bass
from concourse import mybir

P = 128
ALU = mybir.AluOpType
ACT = mybir.ActivationFunctionType
AX = mybir.AxisListType
F32 = mybir.dt.float32
F32R = mybir.dt.float32r
BF16 = mybir.dt.bfloat16

EPS = 1e-5
LORA_SCALE = 4.0
RING = 4
G = 4
CH = 4
DH = 64


class Tile:

    def __init__(self, turn, c):
        self.turn, self.c = turn, c

    def __add__(self, n):
        return Tile(self.turn, self.c + n)

    def __sub__(self, n):
        return Tile(self.turn, self.c - n)

    def count(self, per_tile, more=0):
        return self.turn * (4 * per_tile) + (self.c * per_tile + more)

    def uses(self, by=1):
        return self.turn * by + (self.c // RING) * by

    @property
    def slot(self):
        return self.c % RING

    @property
    def par(self):
        return self.c % 2

    def live(self, tiles):
        return not isinstance(self.turn, int) or 0 <= 4 * self.turn + self.c < tiles


def after(eng, sem, value):
    if not isinstance(value, int) or value > 0:
        eng.wait_ge(sem, value)


def run_slots(nc, eng, first, last, loop_first, loop_last, body):
    turns = (loop_last - loop_first + 1) // 4
    for s in range(first, loop_first):
        body(Tile(0, s))
    with eng.Fori(0, turns) as turn:
        for j in range(4):
            body(Tile(turn, loop_first + j))
    for s in range(loop_first + 4 * turns, last + 1):
        body(Tile(0, s))


def repeat(eng, times, body):
    with eng.Fori(0, times):
        body()


def xattn_lora_moe_kernel(nc, x, ctx_in, router_w, A, B, out):
    NB, C, N = x.shape
    E, R, _ = A.shape
    ER = E * R
    NT = NB * C // P
    NCH = N // P
    W = N // G
    NQ = 96
    assert NCH == G * CH and ER == 64 and ER + E <= NQ and W == 512 and P == 2 * DH

    x_rows = x.rearrange("b c n -> (b c) n")
    ctx_rows = ctx_in.rearrange("b c n -> (b c) n")
    out_rows = out.rearrange("b c n -> (b c) n")

    with ExitStack() as stack:
        def sb(name, shape, dt=F32):
            return stack.enter_context(nc.sbuf_tensor(name, shape, dt))

        def bank(name, shape=(P, 512)):
            return stack.enter_context(nc.psum_tensor(name, list(shape), F32))

        def sem(name):
            return stack.enter_context(nc.semaphore(name))

        ctx_sb = sb("ctx_sb", [P, RING, N])
        x_sb = sb("x_sb", [P, RING, N])
        x1_sb = sb("x1_sb", [P, RING, N])
        q_sb = sb("q_sb", [P, 2, N])
        vT = sb("vT", [P, 2, CH, P + 2])
        ekT = sb("ekT", [P, 2, CH, P])
        attnT = sb("attnT", [P, 2, CH, P])
        x1T = sb("x1T", [P, 2, CH, P])
        kv_bd = sb("kv_bd", [P, 2, 2 * (DH + 1)])
        rden = sb("rden", [P, 2, CH])
        junk = sb("junk", [P, 2, W], BF16)
        kmax_parts = sb("kmax_parts", [P, RING, G])
        kmax = sb("kmax", [P, RING])
        bn_parts = sb("bn_parts", [P, RING, G, 6])
        bn_out = sb("bn_out", [P, RING, 2])
        var1e = sb("var1e", [P, RING])
        rstd1 = sb("rstd1", [P, RING])
        nbias1 = sb("nbias1", [P, RING])
        rz = sb("rz", [P, RING])
        x1_sums = sb("x1_sums", [P, RING, G])
        x1_sum = sb("x1_sum", [P, RING])
        negmean2 = sb("negmean2", [P, RING])
        x1_sq = sb("x1_sq", [P, RING, G])
        var2 = sb("var2", [P, RING])
        var2e = sb("var2e", [P, RING])
        rstd2 = sb("rstd2", [P, RING])
        cen = sb("cen", [P, NQ])
        lmax = sb("lmax", [P, 1])
        lbias = sb("lbias", [P, 1])
        beats = sb("beats", [P, E, 2 * E])
        beats_m = sb("beats_m", [P, E, 2 * E])
        rank = sb("rank", [P, E])
        gexp = sb("gexp", [P, E])
        gsel = sb("gsel", [P, E])
        gsum = sb("gsum", [P, 1])
        grec = sb("grec", [P, 1])
        cen_scaled = sb("cen_scaled", [P, ER])
        mid = sb("mid", [P, ER])
        mid_hl = sb("mid_hl", [P, 2, ER], F32R)
        midT = sb("midT", [P, P], F32R)
        ident = sb("ident", [P, P])
        minus_half = sb("minus_half", [P, 1])
        ones = sb("ones", [P, P])
        order_mask = sb("order_mask", [P, E, 2 * E])
        w_rows = sb("w_rows", [NQ, N])
        wT = sb("wT", [P, NCH, NQ])
        w_row_parts = sb("w_row_parts", [NQ, G])
        w_row_sums = sb("w_row_sums", [NQ, 1])
        w_row_sums_wide = sb("w_row_sums_wide", [NQ, P])
        w_sums = sb("w_sums", [P, NQ])
        b_rows = sb("b_rows", [P, E, NCH, R])
        b_twice = sb("b_twice", [P, NCH, 2, E, R])
        b_hi = sb("b_hi", [P, N], F32R)
        b_lo = sb("b_lo", [P, N], F32R)

        ctxT_ps = bank("ctxT_ps")
        attn_ps = bank("attn_ps")
        x1T_ps = bank("x1T_ps")
        delta_ps = bank("delta_ps")
        kv_ps = bank("kv_ps")
        raw_ps = bank("raw_ps")
        num_ps = bank("num_ps", (P, 2, 512))
        last_delta = [delta_ps, attn_ps, ctxT_ps, kv_ps]
        w_banks = [x1T_ps, delta_ps, raw_ps, x1T_ps]

        ctx_landed = [sem(f"ctx_landed{i}") for i in range(RING)]
        ctx0_landed = [sem(f"ctx0_landed{g}") for g in range(G - 1)]
        x_landed = [sem(f"x_landed{i}") for i in range(RING)]
        out_stored = [sem(f"out_stored{i}") for i in range(RING)]
        w_landed = sem("w_landed")
        r_landed = sem("r_landed")
        b_landed = [sem(f"b_landed{e}") for e in range(E)]
        ident_zeroed = sem("ident_zeroed")
        ident_made = sem("ident_made")
        pool_consts = sem("pool_consts")
        w_pad = sem("w_pad")
        wT_turned = sem("wT_turned")
        wT_copied = sem("wT_copied")
        w_row_parts_made = sem("w_row_parts_made")
        w_row_sums_made = sem("w_row_sums_made")
        w_row_sums_wide_made = sem("w_row_sums_wide_made")
        w_summed = sem("w_summed")
        w_sums_copied = sem("w_sums_copied")
        b_twice_made = sem("b_twice_made")
        b_turned = sem("b_turned")
        b_hi_made = sem("b_hi_made")
        b_lo_made = sem("b_lo_made")
        ctxT_done = sem("ctxT_done")
        kv_done = sem("kv_done")
        num_done = sem("num_done")
        attn_done = sem("attn_done")
        x1T_done = sem("x1T_done")
        raw_done = sem("raw_done")
        midT_done = sem("midT_done")
        delta_done = sem("delta_done")
        tables_loaded = sem("tables_loaded")
        kvT_made = sem("kvT_made")
        q_made = sem("q_made")
        x1T_copied = sem("x1T_copied")
        squares_made = sem("squares_made")
        gexp_made = sem("gexp_made")
        midT_copied = sem("midT_copied")
        kmax_parts_made = sem("kmax_parts_made")
        kmax_made = sem("kmax_made")
        bn_parts_made = sem("bn_parts_made")
        bn_made = sem("bn_made")
        var1e_made = sem("var1e_made")
        rstd1_made = sem("rstd1_made")
        nbias1_made = sem("nbias1_made")
        rz_made = sem("rz_made")
        kv_copied = sem("kv_copied")
        rden_made = sem("rden_made")
        attnT_made = sem("attnT_made")
        x1_made = sem("x1_made")
        x1_sum_made = sem("x1_sum_made")
        negmean2_made = sem("negmean2_made")
        var2_made = sem("var2_made")
        var2e_made = sem("var2e_made")
        rstd2_made = sem("rstd2_made")
        cen_made = sem("cen_made")
        lmax_made = sem("lmax_made")
        lbias_made = sem("lbias_made")
        beats_made = sem("beats_made")
        beats_masked = sem("beats_masked")
        rank_made = sem("rank_made")
        gsel_made = sem("gsel_made")
        grec_made = sem("grec_made")
        cen_scaled_made = sem("cen_scaled_made")
        mid_made = sem("mid_made")
        mid_hi_made = sem("mid_hi_made")
        mid_lo_made = sem("mid_lo_made")
        out_made = sem("out_made")
        ctx0_shifted = sem("ctx0_shifted")
        ctx_shifted = sem("ctx_shifted")

        def cols(g):
            return slice(g * W, (g + 1) * W)

        def is_last(t):
            return isinstance(t.turn, int) and t.c == NT - 1

        def ending(t):
            return isinstance(t.turn, int) and t.c >= NT - 2

        def x1T_bank(t, g):
            return num_ps[:, 0, :] if is_last(t) and g % 2 else x1T_ps[:]

        def delta_bank(t, g):
            return last_delta[g] if ending(t) else delta_ps

        WARM_UP = 10
        POOL_CONSTS = 8 + 2 * (E - 1)

        block = stack.enter_context(nc.Block())

        @block.sync
        def _(sp):
            def load_ctx(t):
                sp.dma_start(ctx_sb[:, t.slot, :], ctx_rows[bass.ts(t.count(1), P), :]).then_inc(ctx_landed[t.slot], 16)

            def load_x(t):
                sp.dma_start(x_sb[:, t.slot, :], x_rows[bass.ts(t.count(1), P), :]).then_inc(x_landed[t.slot], 16)

            for g in range(G):
                landed = ctx0_landed[g] if g < G - 1 else ctx_landed[0]
                sp.dma_start(ctx_sb[:, 0, cols(g)], ctx_rows[0:P, cols(g)]).then_inc(landed, 16)
            load_ctx(Tile(0, 1))
            load_x(Tile(0, 0))
            load_ctx(Tile(0, 2))
            load_x(Tile(0, 1))
            sp.wait_ge(w_pad, 1)
            sp.dma_start(w_rows[ER:ER + E, :], router_w).then_inc(r_landed, 16)
            sp.dma_start(w_rows[0:ER, :], A.rearrange("e r n -> (e r) n")).then_inc(w_landed, 16)
            load_ctx(Tile(0, 3))
            for e in range(E):
                sp.dma_start(b_rows[:, e, :, :], B[e].rearrange("(p j) r -> p j r", j=NCH)).then_inc(b_landed[e], 16)
            load_x(Tile(0, 2))
            load_x(Tile(0, 3))

            def slot(s):
                if (s - 4).live(NT):
                    t = s - 4
                    if ending(t):
                        for g in range(G):
                            sp.wait_ge(out_made, t.count(G, g + 1))
                            sp.dma_start(out_rows[t.c * P:(t.c + 1) * P, cols(g)],
                                         x1_sb[:, t.slot, cols(g)]).then_inc(out_stored[t.slot], 16)
                        return
                    after(sp, out_made, t.count(G, G))
                    sp.dma_start(out_rows[bass.ts(t.count(1), P), :], x1_sb[:, t.slot, :]).then_inc(out_stored[t.slot], 16)
                if (s + 4).live(NT):
                    if s.live(NT):
                        after(sp, ctxT_done, s.count(G, G))
                    load_ctx(s + 4)
                if (s + 3).live(NT) and (s - 1).live(NT):
                    after(sp, x1_made, (s - 1).count(G, G))
                    load_x(s + 3)

            run_slots(nc, sp, 0, NT + 3, 4, NT - 5, slot)
            for i in range(RING):
                sp.wait_ge(out_stored[i], 16 * (NT // RING + (G - 1 if ending(Tile(0, NT - RING + i)) else 0)))

        @block.gpsimd
        def _(pool):
            pool.memset(ident[:], 0.0).then_inc(ident_zeroed, 1)
            pool.wait_ge(ident_zeroed, 1)
            pool.affine_select(out=ident[:], in_=ident[:], compare_op=ALU.not_equal, fill=1.0, base=0,
                               pattern=[[-1, P]], channel_multiplier=1).then_inc(ident_made, 1)
            pool.wait_ge(ident_made, 1)
            order = order_mask
            fills = [(ones[:], 1.0), (vT[:, 0, :, P:P + 2], 1.0), (vT[:, 1, :, P:P + 2], 1.0), (kv_bd[:], 0.0),
                     (minus_half[:], -0.5), (order[:], 0.0)]
            fills += [(kv_bd[h * DH:(h + 1) * DH, :, h * (DH + 1) + DH:h * (DH + 1) + DH + 1], 1.0) for h in range(2)]
            fills += [(order[:, e, e + 1:E], 1.0) for e in range(E - 1)]
            fills += [(order[:, e, E:E + e], 1.0) for e in range(1, E)]
            assert len(fills) == POOL_CONSTS
            for n, (what, value) in enumerate(fills):
                if n >= 1:
                    pool.wait_ge(pool_consts, n)
                pool.memset(what, value).then_inc(pool_consts, 1)

            def b_twice_parts():
                for e in range(E):
                    pool.wait_ge(b_landed[e], 16)
                for d in range(2):
                    pool.tensor_copy(b_twice[:, :, d, :, :],
                                     b_rows[:].rearrange("p e j r -> p j e r")).then_inc(b_twice_made, 1)

            def root(t, var, rstd, ready, made):
                if t.live(NT):
                    after(pool, ready, t.count(1, 1))
                    pool.tensor_tensor(rstd[:, t.slot:t.slot + 1], var[:, t.slot:t.slot + 1], minus_half[:],
                                       ALU.pow).then_inc(made, 1)

            def slot(s):
                root(s - 3, var2e, rstd2, var2e_made, rstd2_made)
                early = isinstance(s.turn, int)
                if early and s.c in (-1, 0):
                    shift_ctx(s + 2)
                elif not (early and s.c == 1):
                    shift_ctx(s + 1)
                if early and s.c == 1:
                    b_twice_parts()
                root(s + 1, var1e, rstd1, var1e_made, rstd1_made)

            def shift_ctx(t):
                if t.live(NT):
                    after(pool, kmax_made, t.count(1, 1))
                    pool.tensor_tensor(ctx_sb[:, t.slot, :], ctx_sb[:, t.slot, :],
                                       kmax[:, t.slot:t.slot + 1].to_broadcast([P, N]),
                                       ALU.subtract).then_inc(ctx_shifted, 1)

            run_slots(nc, pool, -1, NT + 2, 4, NT - 2, slot)

        @block.tensor
        def _(pe):
            pe.wait_ge(ident_made, 1)
            def turn_identity():
                for _ in range(4):
                    pe.transpose(raw_ps[:, 0:P], ident[:], ident[:])
            repeat(pe, WARM_UP, turn_identity)

            def turn_w():
                pe.wait_ge(w_landed, 16)
                pe.wait_ge(r_landed, 16)
                for g in range(G):
                    if g >= 3:
                        pe.wait_ge(wT_copied, g - 2)
                    for j in range(CH):
                        c = g * CH + j
                        mm = pe.transpose(w_banks[g][:, j * NQ:(j + 1) * NQ], w_rows[:, c * P:(c + 1) * P],
                                          ident[0:NQ, 0:NQ])
                    mm.then_inc(wT_turned, 1)

            def spread_w_sums():
                pe.wait_ge(w_row_sums_wide_made, 1)
                pe.wait_ge(wT_copied, G)
                pe.matmul(delta_ps[:, 0:NQ], w_row_sums_wide[:], ident[0:NQ, 0:NQ], start=True,
                          stop=True).then_inc(w_summed, 1)

            def turn_b(g):
                if g == 0:
                    pe.wait_ge(b_twice_made, 2)
                    pe.wait_ge(w_sums_copied, 1)
                else:
                    pe.wait_ge(b_lo_made, g)
                for j in range(CH):
                    mm = pe.transpose(delta_ps[:, j * P:(j + 1) * P],
                                      b_twice[:, g * CH + j, :, :, :].rearrange("p d e r -> p (d e r)"), ident[:])
                mm.then_inc(b_turned, 1)

            def turn_ctx(t, g):
                if not t.live(NT):
                    return
                if isinstance(t.turn, int) and t.c == 0 and g < G - 1:
                    pe.wait_ge(ctx0_shifted, g + 1)
                elif g == 0 or isinstance(t.turn, int) and t.c == 0:
                    after(pe, ctx_shifted, t.count(1, 1))
                after(pe, kvT_made, t.count(2 * G, 2 * g))
                for j in range(CH):
                    c = g * CH + j
                    mm = pe.transpose(ctxT_ps[:, j * P:(j + 1) * P], ctx_sb[:, t.slot, c * P:(c + 1) * P], ident[:])
                mm.then_inc(ctxT_done, 1)

            def kv(t, g):
                if not t.live(NT):
                    return
                if g == 0:
                    after(pe, kv_copied, t.count(2))
                after(pe, kvT_made, t.count(2 * G, 2 * g + 2))
                for j in range(CH):
                    mm = pe.matmul(kv_ps[:, 0:P + 2], ekT[:, g % 2, j, :], vT[:, g % 2, j, :],
                                   start=(g == 0 and j == 0), stop=(g == G - 1 and j == CH - 1))
                mm.then_inc(kv_done, 1)

            def numerator(t, g):
                if not t.live(NT):
                    return
                if g == 0:
                    after(pe, kv_copied, t.count(2, 2))
                after(pe, q_made, t.count(G, g + 1))
                after(pe, attnT_made, t.count(G, g))
                for j in range(CH):
                    c = g * CH + j
                    at = (j % 2) * 2 * (DH + 1)
                    mm = pe.matmul(num_ps[:, j // 2, at:at + 2 * (DH + 1)], q_sb[:, t.par, c * P:(c + 1) * P],
                                   kv_bd[:, t.par, :], start=True, stop=True)
                mm.then_inc(num_done, 1)

            def turn_attn(t, g):
                if not t.live(NT):
                    return
                after(pe, attnT_made, t.count(G, g + 1))
                after(pe, x1_made, t.count(G, g))
                for j in range(CH):
                    mm = pe.transpose(attn_ps[:, j * P:(j + 1) * P], attnT[:, g % 2, j, :], ident[:])
                mm.then_inc(attn_done, 1)

            def turn_x1(t, g):
                if not t.live(NT):
                    return
                after(pe, x1_made, t.count(G, g + 1))
                after(pe, x1T_copied, t.count(G, g - 1 if is_last(t) and g else g))
                for j in range(CH):
                    c = g * CH + j
                    mm = pe.transpose(x1T_bank(t, g)[:, j * P:(j + 1) * P], x1_sb[:, t.slot, c * P:(c + 1) * P], ident[:])
                mm.then_inc(x1T_done, 1)

            def project(t, g):
                if not t.live(NT):
                    return
                if g == 0:
                    after(pe, cen_made, t.count(1))
                after(pe, x1T_copied, t.count(G, g + 1))
                for j in range(CH):
                    mm = pe.matmul(raw_ps[:, 0:NQ], x1T[:, g % 2, j, :], wT[:, g * CH + j, :],
                                   start=(g == 0 and j == 0), stop=(g == G - 1 and j == CH - 1))
                mm.then_inc(raw_done, 1)

            def turn_mid(t):
                if not t.live(NT):
                    return
                after(pe, mid_lo_made, t.count(1, 1))
                after(pe, out_made, (t - 1).count(G, 1) if ending(t - 1) else t.count(G))
                pe.transpose(delta_ps[:, 0:P], mid_hl[:].rearrange("p d m -> p (d m)").bitcast(F32),
                             ident[:]).then_inc(midT_done, 1)

            def delta(t, g):
                if not t.live(NT):
                    return
                after(pe, midT_copied, t.count(1, 1))
                ps = delta_bank(t, g)
                if not ending(t):
                    after(pe, out_made, t.count(G, g))
                elif ending(t - 1):
                    pe.wait_ge(out_made, (t - 1).count(G, g + 1))
                pe.matmul(ps[:], midT[:], b_hi[:, cols(g)], start=True, stop=False)
                pe.matmul(ps[:], midT[:], b_lo[:, cols(g)], start=False, stop=True).then_inc(delta_done, 1)

            def slot(s):
                early = isinstance(s.turn, int)
                if early and s.c == 3:
                    pe.wait_ge(b_lo_made, G)
                for g in range(G):
                    turn_ctx(s, g)
                    if g >= 1:
                        kv(s, g - 1)
                    turn_x1(s - 2, g)
                    if early and s.c == 1 and g == 2:
                        turn_w()
                    if g >= 1:
                        project(s - 2, g - 1)
                        turn_attn(s - 1, g - 1)
                    if g == 2 and not is_last(s - 2):
                        turn_mid(s - 3)
                    numerator(s - 1, g)
                    if g == (1 if is_last(s - 2) else 0) and not ending(s - 4):
                        delta(s - 4, G - 1)
                    if g >= 2 and not ending(s - 3):
                        delta(s - 3, g - 2)
                    if early and s.c == 2:
                        if g == 0:
                            spread_w_sums()
                        turn_b(g)
                kv(s, G - 1)
                project(s - 2, G - 1)
                turn_attn(s - 1, G - 1)
                if is_last(s - 2):
                    turn_mid(s - 3)
                if ending(s - 3):
                    for g in range(G):
                        delta(s - 3, g)
                else:
                    delta(s - 3, G - 2)
            run_slots(nc, pe, 0, NT + 3, 4, NT - 1, slot)

        @block.scalar
        def _(act):
            def copy_wT():
                for g in range(G):
                    act.wait_ge(wT_turned, g + 1)
                    act.activation(wT[:, g * CH:(g + 1) * CH, :],
                                   w_banks[g][:, 0:CH * NQ].rearrange("p (j w) -> p j w", j=CH),
                                   ACT.Copy).then_inc(wT_copied, 1)

            def sum_w(g):
                if g == 0:
                    act.wait_ge(w_landed, 16)
                    act.wait_ge(r_landed, 16)
                after(act, w_row_parts_made, g)
                act.activation(junk[0:NQ, g % 2, :], w_rows[:, cols(g)], ACT.Copy,
                               accum_out=w_row_parts[:, g:g + 1]).then_inc(w_row_parts_made, 1)

            def copy_w_sums():
                act.wait_ge(w_summed, 1)
                act.activation(w_sums[:], delta_ps[:, 0:NQ], ACT.Copy).then_inc(w_sums_copied, 1)

            def b_high(g):
                act.wait_ge(b_turned, g + 1)
                act.activation(b_hi[:].rearrange("k (p j) -> k j p", j=NCH)[:, g * CH:(g + 1) * CH, :],
                               delta_ps[:].rearrange("k (j p) -> k j p", j=CH), ACT.Copy).then_inc(b_hi_made, 1)

            def transposed_ctx(t, g):
                if not t.live(NT):
                    return
                after(act, ctxT_done, t.count(G, g + 1))
                after(act, kv_done, t.count(G, g - 1))
                act.activation(vT[:, g % 2, :, 0:P], ctxT_ps[:].rearrange("p (j c) -> p j c", j=CH),
                               ACT.Copy).then_inc(kvT_made, 1)
                act.activation(ekT[:, g % 2, :, :], ctxT_ps[:].rearrange("p (j c) -> p j c", j=CH),
                               ACT.Exp).then_inc(kvT_made, 1)

            def query(t, g):
                if not t.live(NT):
                    return
                if g == 0:
                    after(act, nbias1_made, t.count(1, 1))
                after(act, num_done, (t - 2).count(G, g + 1))
                act.activation(q_sb[:, t.par, cols(g)], x_sb[:, t.slot, cols(g)], ACT.Exp,
                               bias=nbias1[:, t.slot:t.slot + 1],
                               scale=rstd1[:, t.slot:t.slot + 1]).then_inc(q_made, 1)

            def copy_x1T(t, g):
                if not t.live(NT):
                    return
                after(act, x1T_done, t.count(G, g + 1))
                after(act, raw_done, t.count(G, g - 1))
                act.activation(x1T[:, g % 2, :, :], x1T_bank(t, g).rearrange("p (j c) -> p j c", j=CH),
                               ACT.Copy).then_inc(x1T_copied, 1)

            def square(t, g):
                if not t.live(NT):
                    return
                if g == 0:
                    after(act, negmean2_made, t.count(1, 1))
                if isinstance(t.turn, int) and t.c == 0 and g == 0:
                    act.wait_ge(w_row_parts_made, G)
                after(act, squares_made, t.count(G, g - 1))
                act.activation(junk[:, g % 2, :], x1_sb[:, t.slot, cols(g)], ACT.Square,
                               bias=negmean2[:, t.slot:t.slot + 1],
                               accum_out=x1_sq[:, t.slot, g:g + 1]).then_inc(squares_made, 1)

            def copy_kv(t):
                if not t.live(NT):
                    return
                after(act, rz_made, t.count(1, 1))
                after(act, num_done, (t - 1).count(G))
                for h in range(2):
                    rows = slice(h * DH, (h + 1) * DH)
                    act.activation(kv_bd[rows, t.par, h * (DH + 1):h * (DH + 1) + DH], kv_ps[rows, h * DH:(h + 1) * DH],
                                   ACT.Copy, scale=rz[rows, t.slot:t.slot + 1]).then_inc(kv_copied, 1)

            def gate_exp(t):
                if not t.live(NT):
                    return
                after(act, lbias_made, t.count(1, 1))
                act.activation(gexp[:], cen[:, ER:ER + E], ACT.Exp, bias=lbias[:, 0:1],
                               scale=rstd2[:, t.slot:t.slot + 1]).then_inc(gexp_made, 1)

            def copy_midT(t):
                if not t.live(NT):
                    return
                after(act, midT_done, t.count(1, 1))
                after(act, delta_done, t.count(G))
                act.activation(midT[:], delta_ps[:, 0:P], ACT.Copy).then_inc(midT_copied, 1)

            def slot(s):
                early = isinstance(s.turn, int)
                if is_last(s - 2):
                    copy_x1T(s - 2, 0)
                    copy_x1T(s - 2, 1)
                    gate_exp(s - 3)
                    square(s - 2, 0)
                    copy_x1T(s - 2, 2)
                    square(s - 2, 1)
                    copy_x1T(s - 2, 3)
                    square(s - 2, 2)
                    square(s - 2, 3)
                    copy_midT(s - 3)
                    return
                for g in range(G):
                    transposed_ctx(s, g)
                    copy_x1T(s - 2, g)
                    if early and s.c == 2 and g == 0:
                        copy_w_sums()
                    if g == 2:
                        copy_midT(s - 3)
                    if early and s.c == 1:
                        if g < 2:
                            query(s - 1, 2 + g)
                        else:
                            query(s, g - 2)
                        if g == 1:
                            copy_wT()
                        if g >= 2:
                            sum_w(2 * g - 4)
                            sum_w(2 * g - 3)
                    elif not (early and s.c == 0):
                        query(s, g)
                    if g == 0:
                        gate_exp(s - 3)
                    square(s - 2, g)
                    if early and s.c == 2:
                        b_high(g)
                if early and s.c == 0:
                    query(s, 0)
                copy_kv(s)
                if early and s.c == 0:
                    query(s, 1)
                if early and s.c == 1:
                    query(s, 2)
                    query(s, 3)

            act.wait_ge(ident_made, 1)
            act.activation(junk[:, 0, 0:P], ident[:], ACT.Exp).then_inc(tables_loaded, 1)
            act.wait_ge(tables_loaded, 1)
            act.wait_ge(pool_consts, POOL_CONSTS)
            run_slots(nc, act, 0, NT + 2, 4, NT - 1, slot)

        @block.vector
        def _(dve):
            def spread_w_row_sums():
                dve.wait_ge(w_row_parts_made, G)
                dve.tensor_reduce(w_row_sums[:], w_row_parts[:], AX.X, ALU.add).then_inc(w_row_sums_made, 1)
                dve.wait_ge(pool_consts, POOL_CONSTS)
                dve.wait_ge(w_row_sums_made, 1)
                dve.tensor_scalar(w_row_sums_wide[:], ones[0:NQ, :], w_row_sums[:, 0:1], None,
                                  ALU.mult).then_inc(w_row_sums_wide_made, 1)

            def b_low(g):
                dve.wait_ge(b_hi_made, g + 1)
                hi = b_hi[:].rearrange("k (p j) -> k j p", j=NCH)[:, g * CH:(g + 1) * CH, :]
                lo = b_lo[:].rearrange("k (p j) -> k j p", j=NCH)[:, g * CH:(g + 1) * CH, :]
                dve.tensor_tensor(lo, delta_ps[:].rearrange("k (j p) -> k j p", j=CH), hi,
                                  ALU.subtract).then_inc(b_lo_made, 1)

            def max_part(t, g):
                if not t.live(NT):
                    return
                if isinstance(t.turn, int) and t.c == 0:
                    dve.wait_ge(ctx0_landed[g] if g < G - 1 else ctx_landed[0], 16)
                elif g == 0:
                    after(dve, ctx_landed[t.slot], t.uses(16) + 16)
                dve.tensor_reduce(kmax_parts[:, t.slot, g:g + 1], ctx_sb[:, t.slot, cols(g)], AX.X,
                                  ALU.max).then_inc(kmax_parts_made, 1)

            def max_whole(t):
                if not t.live(NT):
                    return
                after(dve, kmax_parts_made, t.count(G, G))
                dve.tensor_reduce(kmax[:, t.slot:t.slot + 1], kmax_parts[:, t.slot, :], AX.X,
                                  ALU.max).then_inc(kmax_made, 1)

            def bn_part(t, g):
                if not t.live(NT):
                    return
                if g == 0:
                    after(dve, x_landed[t.slot], t.uses(16) + 16)
                dve.bn_stats(bn_parts[:, t.slot, g, :], x_sb[:, t.slot, cols(g)]).then_inc(bn_parts_made, 1)

            def ln1(t, step):
                if not t.live(NT):
                    return
                i = t.slot
                if step == 0:
                    dve.bn_aggr(bn_out[:, i, :], bn_parts[:, i, :, :].rearrange("p g s -> p (g s)")).then_inc(bn_made, 1)
                if step == 1:
                    after(dve, bn_made, t.count(1, 1))
                    dve.tensor_scalar(var1e[:, i:i + 1], bn_out[:, i, 1:2], EPS, None, ALU.add).then_inc(var1e_made, 1)
                if step == 2:
                    after(dve, rstd1_made, t.count(1, 1))
                    dve.tensor_scalar(nbias1[:, i:i + 1], bn_out[:, i, 0:1], rstd1[:, i:i + 1], -1.0, ALU.mult,
                                      ALU.mult).then_inc(nbias1_made, 1)

            def bn_all(t):
                if t.live(NT):
                    after(dve, bn_parts_made, t.count(G, G))

            def kv_recip(t):
                if not t.live(NT):
                    return
                after(dve, kv_done, t.count(G, G))
                dve.reciprocal(rz[:, t.slot:t.slot + 1], kv_ps[:, P:P + 1]).then_inc(rz_made, 1)

            heads = num_ps[:, :, 0:4 * (DH + 1)].rearrange("p b (k w) -> p b k w", w=DH + 1)

            def den_recip(t, g):
                if not t.live(NT):
                    return
                after(dve, num_done, t.count(G, g + 1))
                dve.reciprocal(rden[:], heads[:, :, :, DH]).then_inc(rden_made, 1)

            def normalise(t, g):
                if not t.live(NT):
                    return
                after(dve, rden_made, t.count(G, g + 1))
                after(dve, attn_done, t.count(G, g - 1))
                dve.tensor_tensor(attnT[:, g % 2, :, :].rearrange("p (b j) (h d) -> p b (j h) d", b=2, h=2),
                                  heads[:, :, :, 0:DH], rden[:].unsqueeze(3).to_broadcast([P, 2, CH, DH]),
                                  ALU.mult).then_inc(attnT_made, 1)

            def add_x(t, g):
                if not t.live(NT):
                    return
                if g == 0:
                    after(dve, out_stored[t.slot], t.uses(16))
                after(dve, attn_done, t.count(G, g + 1))
                dve.scalar_tensor_tensor(out=x1_sb[:, t.slot, cols(g)], in0=attn_ps[:], scalar=kmax[:, t.slot:t.slot + 1],
                                         in1=x_sb[:, t.slot, cols(g)], op0=ALU.add, op1=ALU.add,
                                         accum_out=x1_sums[:, t.slot, g:g + 1]).then_inc(x1_made, 1)

            def mean2(t, step):
                if not t.live(NT):
                    return
                i = t.slot
                if step == 0:
                    after(dve, x1_made, t.count(G, G))
                    dve.tensor_reduce(x1_sum[:, i:i + 1], x1_sums[:, i, :], AX.X, ALU.add).then_inc(x1_sum_made, 1)
                if step == 1:
                    after(dve, x1_sum_made, t.count(1, 1))
                    dve.tensor_scalar(negmean2[:, i:i + 1], x1_sum[:, i:i + 1], -1.0 / N, None,
                                      ALU.mult).then_inc(negmean2_made, 1)

            def gate(t, step):
                if not t.live(NT):
                    return
                i = t.slot
                lg = cen[:, ER:ER + E]
                them = lg.unsqueeze(1).to_broadcast([P, E, E])
                it = lg.unsqueeze(2).to_broadcast([P, E, E])
                if step == "variance sum":
                    after(dve, squares_made, t.count(G, G))
                    dve.tensor_reduce(var2[:, i:i + 1], x1_sq[:, i, :], AX.X, ALU.add).then_inc(var2_made, 1)
                if step == "centre":
                    after(dve, raw_done, t.count(G, G))
                    dve.scalar_tensor_tensor(out=cen[:], in0=w_sums[:], scalar=negmean2[:, i:i + 1],
                                             in1=raw_ps[:, 0:NQ], op0=ALU.mult, op1=ALU.add).then_inc(cen_made, 1)
                if step == "variance":
                    after(dve, var2_made, t.count(1, 1))
                    dve.tensor_scalar(var2e[:, i:i + 1], var2[:, i:i + 1], 1.0 / N, EPS, ALU.mult,
                                      ALU.add).then_inc(var2e_made, 1)
                if step == "logit maximum":
                    after(dve, cen_made, t.count(1, 1))
                    dve.tensor_reduce(lmax[:], lg, AX.X, ALU.max).then_inc(lmax_made, 1)
                if step == "greater":
                    dve.tensor_tensor(beats[:, :, 0:E], them, it, ALU.is_gt).then_inc(beats_made, 1)
                if step == "logit bias":
                    after(dve, rstd2_made, t.count(1, 1))
                    after(dve, lmax_made, t.count(1, 1))
                    dve.tensor_scalar(lbias[:], lmax[:], rstd2[:, i:i + 1], -1.0, ALU.mult,
                                      ALU.mult).then_inc(lbias_made, 1)
                if step == "greater or equal":
                    dve.tensor_tensor(beats[:, :, E:2 * E], them, it, ALU.is_ge).then_inc(beats_made, 1)
                if step == "mask":
                    after(dve, beats_made, t.count(2, 2))
                    dve.tensor_tensor(beats_m[:], beats[:], order_mask[:], ALU.mult).then_inc(beats_masked, 1)
                if step == "rank":
                    after(dve, beats_masked, t.count(1, 1))
                    dve.tensor_reduce(rank[:], beats_m[:], AX.X, ALU.add).then_inc(rank_made, 1)
                if step == "select":
                    after(dve, rank_made, t.count(1, 1))
                    after(dve, gexp_made, t.count(1, 1))
                    dve.scalar_tensor_tensor(out=gsel[:], in0=rank[:], scalar=2.0, in1=gexp[:], op0=ALU.is_lt,
                                             op1=ALU.mult, accum_out=gsum[:]).then_inc(gsel_made, 1)
                if step == "over sum":
                    after(dve, gsel_made, t.count(1, 1))
                    dve.reciprocal(grec[:], gsum[:]).then_inc(grec_made, 1)
                if step == "scaled middle":
                    dve.tensor_scalar(cen_scaled[:], cen[:, 0:ER], rstd2[:, i:i + 1], LORA_SCALE, ALU.mult,
                                      ALU.mult).then_inc(cen_scaled_made, 1)
                if step == "middle":
                    after(dve, cen_scaled_made, t.count(1, 1))
                    after(dve, grec_made, t.count(1, 1))
                    dve.scalar_tensor_tensor(out=mid[:].rearrange("p (e r) -> p e r", e=E),
                                             in0=cen_scaled[:].rearrange("p (e r) -> p e r", e=E),
                                             scalar=grec[:, 0:1], in1=gsel[:].unsqueeze(2).to_broadcast([P, E, R]),
                                             op0=ALU.mult, op1=ALU.mult).then_inc(mid_made, 1)
                if step == "high part":
                    after(dve, mid_made, t.count(1, 1))
                    after(dve, midT_done, t.count(1))
                    dve.tensor_copy(mid_hl[:, 0, :], mid[:]).then_inc(mid_hi_made, 1)
                if step == "low part":
                    after(dve, mid_hi_made, t.count(1, 1))
                    dve.tensor_tensor(mid_hl[:, 1, :], mid[:], mid_hl[:, 0, :], ALU.subtract).then_inc(mid_lo_made, 1)

            def add_delta(t, g):
                if not t.live(NT):
                    return
                after(dve, delta_done, t.count(G, g + 1))
                dve.tensor_tensor(x1_sb[:, t.slot, cols(g)], delta_bank(t, g)[:], x1_sb[:, t.slot, cols(g)],
                                  ALU.add).then_inc(out_made, 1)

            def slot(s):
                early = isinstance(s.turn, int)
                if early and s.c <= 0:
                    first_slots(s)
                    return
                if early and s.c == NT + 2:
                    last_gates(s - 3)
                    return
                gate(s - 3, "variance sum")
                gate(s - 3, "centre")
                if not (early and s.c == 1):
                    ln1(s, 2)
                gate(s - 3, "variance")
                gate(s - 3, "logit maximum")
                gate(s - 3, "greater")
                den_recip(s - 1, 0)
                if not (early and s.c == 1):
                    max_part(s + 2, 0)
                normalise(s - 1, 0)
                if early and s.c == 1:
                    bn_part(s, 2)
                    bn_part(s, 3)
                    bn_all(s)
                    ln1(s, 0)
                gate(s - 3, "logit bias")
                gate(s - 3, "greater or equal")
                gate(s - 3, "scaled middle")
                if not ending(s - 4):
                    add_delta(s - 4, G - 1)
                gate(s - 3, "mask")
                if not (early and s.c == 1):
                    bn_part(s + 1, 0)
                if early and s.c == 2:
                    b_low(0)
                if early and s.c == 1:
                    ln1(s, 1)
                gate(s - 3, "rank")
                add_x(s - 1, 0)
                if early and s.c == 1:
                    max_part(s + 2, 0)
                gate(s - 3, "select")
                den_recip(s - 1, 1)
                gate(s - 3, "over sum")
                normalise(s - 1, 1)
                if early and s.c == 1:
                    ln1(s, 2)
                gate(s - 3, "middle")
                gate(s - 3, "high part")
                max_part(s + 2, 1)
                gate(s - 3, "low part")
                if early and s.c == 2:
                    b_low(1)
                add_x(s - 1, 1)
                if early and s.c == 1:
                    bn_part(s + 1, 0)
                bn_part(s + 1, 1)
                den_recip(s - 1, 2)
                max_part(s + 2, 2)
                normalise(s - 1, 2)
                if not ending(s - 3):
                    add_delta(s - 3, 0)
                max_part(s + 2, 3)
                bn_part(s + 1, 2)
                if early and s.c == 2:
                    b_low(2)
                add_x(s - 1, 2)
                den_recip(s - 1, 3)
                max_whole(s + 2)
                bn_part(s + 1, 3)
                if early and s.c == 2:
                    b_low(3)
                normalise(s - 1, 3)
                if not ending(s - 3):
                    add_delta(s - 3, 1)
                bn_all(s + 1)
                kv_recip(s)
                ln1(s + 1, 0)
                add_x(s - 1, 3)
                ln1(s + 1, 1)
                mean2(s - 1, 0)
                if not ending(s - 3):
                    add_delta(s - 3, 2)
                mean2(s - 1, 1)
                if early and s.c == 1:
                    spread_w_row_sums()
                if early and s.c == 2:
                    dve.wait_ge(pool_consts, POOL_CONSTS)
                    dve.wait_ge(w_sums_copied, 1)

            def first_slots(s):
                t = s + 2
                max_part(t, 0)
                if s.c == 0:
                    ln1(s, 2)
                max_part(t, 1)
                max_part(t, 2)
                if s.c == 0:
                    kv_recip(s)
                max_part(t, 3)
                max_whole(t)
                if s.c == -2:
                    dve.wait_ge(kmax_made, 1)
                    for g in range(G):
                        dve.tensor_scalar(ctx_sb[:, 0, cols(g)], ctx_sb[:, 0, cols(g)], kmax[:, 0:1], None,
                                          ALU.subtract).then_inc(ctx0_shifted if g < G - 1 else ctx_shifted, 1)
                if s.c == -1:
                    for g in range(G):
                        bn_part(s + 1, g)
                    bn_all(s + 1)
                    ln1(s + 1, 0)
                    ln1(s + 1, 1)
                if s.c == 0:
                    bn_part(s + 1, 0)
                    bn_part(s + 1, 1)

            def last_gates(t):
                gate(t, "centre")
                gate(t, "variance sum")
                gate(t, "logit maximum")
                gate(t, "greater")
                gate(t, "variance")
                gate(t, "greater or equal")
                gate(t, "logit bias")
                gate(t, "mask")
                gate(t, "scaled middle")
                add_delta(t - 1, 0)
                gate(t, "rank")
                gate(t, "select")
                add_delta(t - 1, 1)
                gate(t, "over sum")
                gate(t, "middle")
                gate(t, "high part")
                gate(t, "low part")
                for g in (2, 3):
                    add_delta(t - 1, g)
                for g in range(G):
                    add_delta(t, g)

            dve.memset(w_rows[ER:NQ, :], 0.0).then_inc(w_pad, 1)
            run_slots(nc, dve, -2, NT + 3, 5, NT - 3, slot)


_INS = ["x", "ctx_4096", "L0_ffn_router_w", "L0_ffn_A", "L0_ffn_B"]
_OUTS = [((8, 512, 2048), "float32")]


def kernel(**inputs):
    import numpy as _np
    import concourse.bacc as _bacc
    from concourse import mybir as _mybir
    from concourse.bass_utils import run_bass_kernel_spmd as _run

    nc = _bacc.Bacc("TRN2", target_bir_lowering=False, num_devices=1)
    arrays, args = {}, []
    for name in _INS:
        a = _np.ascontiguousarray(inputs[name])
        arrays[f"in_{name}_dram"] = a
        args.append(nc.dram_tensor(f"in_{name}_dram", a.shape, _mybir.dt.from_np(a.dtype), kind="ExternalInput").ap())
    for i, (shape, dtype) in enumerate(_OUTS):
        dt = _mybir.dt.from_np(_np.dtype(dtype))
        args.append(nc.dram_tensor(f"out_{i}_dram", shape, dt, kind="ExternalOutput").ap())
    xattn_lora_moe_kernel(nc, *args)
    r = _run(nc, [arrays], core_ids=[0])
    return r.results[0]["out_0_dram"]
```
